# Optimizing a Trainium2 kernel written in Bass

```python
import numpy as np
import jax
import jax.numpy as jnp

def _softmax(x, axis=-1):
    return jax.nn.softmax(x, axis=axis)

def _gelu(x):
    return jax.nn.gelu(x, approximate=True)

def _silu(x):
    return jax.nn.silu(x)

def _sigmoid(x):
    return jax.nn.sigmoid(x)

def _layernorm(x, axis=-1, eps=1e-05):
    m = jnp.mean(x, axis=axis, keepdims=True)
    v = jnp.var(x, axis=axis, keepdims=True)
    return (x - m) / jnp.sqrt(v + eps)

def _scatter_add(tgt, idx, src, axis=0):
    return tgt.at[idx].add(src)

def _segment_sum(src, seg, n):
    return jax.ops.segment_sum(src, seg, n)
kernel_name = 'mk_xattn_seq_d1_seqx_r8_062081'

def setup_inputs(seed: int=0):
    np.random.seed(seed)
    _w = jnp.asarray

    def _rec_inputs():
        import jax
        import jax.numpy as jnp
        _rk = jax.random.key(seed)
        x = 7.22e-05 + 1 * jax.random.normal(jax.random.fold_in(_rk, 1), (32, 64, 256), jnp.float32)
        _lenS = 64 - jax.random.randint(jax.random.fold_in(_rk, 7), (32,), 0, max(1, 64 // 4) + 1, jnp.int32)
        _lenS2 = 64 - jax.random.randint(jax.random.fold_in(_rk, 8), (32,), 0, max(1, 64 // 4) + 1, jnp.int32)
        _ctx_2048P = jax.random.normal(jax.random.fold_in(_rk, 11), (32, 16, 256), jnp.float32)
        _ctx_2048c = jax.random.dirichlet(jax.random.fold_in(_rk, 511), 0.3 * jnp.ones((16,), jnp.float32), (32, 64))
        _ctx_2048t = jnp.einsum('bsk,bkd->bsd', _ctx_2048c, _ctx_2048P)
        _ctx_2048t = _ctx_2048t * jax.lax.rsqrt(jnp.mean(jnp.square(_ctx_2048t)) + 1e-12) * 0.953939
        ctx_2048 = 2.81802e-05 + 1.00001 * (_ctx_2048t + 0.3 * jax.random.normal(jax.random.fold_in(_rk, 611), (32, 64, 256), jnp.float32))
        _validS = jnp.arange(64)[None, :] < _lenS[:, None]
        _validS2 = jnp.arange(64)[None, :] < _lenS2[:, None]
        _causal = jnp.tril(jnp.ones((64, 64), dtype=bool))
        mask_BxS2_bf1 = jnp.ones((32, 64), dtype=bool)
        return (x, ctx_2048, mask_BxS2_bf1)
    x, ctx_2048, mask_BxS2_bf1 = _rec_inputs()

    def _L0_xattn_setup():
        import jax, jax.numpy as jnp
        import numpy as np
        D = 256
        H = 16
        HD = D // H
        INNER = 4 * D
        EPS = 1e-05

        def layer_norm(x, w, b):
            mu = jnp.mean(x, axis=-1, keepdims=True)
            var = jnp.mean(jnp.square(x - mu), axis=-1, keepdims=True)
            return (x - mu) * jax.lax.rsqrt(var + EPS) * w + b
        key = jax.random.key(seed)
        ks = jax.random.split(key, 12)
        B, LQ, LK = (4, 128, 256)
        std = 0.02
        inp = {'hidden_states': jax.random.normal(ks[0], (B, LQ, D), jnp.float32), 'encoder_hidden_states': jax.random.normal(ks[1], (B, LK, D), jnp.float32), 'encoder_attention_mask': jnp.ones((B, LK), dtype=bool), 'ln1_w': jnp.ones((D,), jnp.float32), 'ln1_b': jnp.zeros((D,), jnp.float32), 'q_w': jax.random.normal(ks[2], (D, D), jnp.float32) * std, 'q_b': jnp.zeros((D,), jnp.float32), 'k_w': jax.random.normal(ks[3], (D, D), jnp.float32) * std, 'k_b': jnp.zeros((D,), jnp.float32), 'v_w': jax.random.normal(ks[4], (D, D), jnp.float32) * std, 'v_b': jnp.zeros((D,), jnp.float32), 'cproj_w': jax.random.normal(ks[5], (D, D), jnp.float32) * std, 'cproj_b': jnp.zeros((D,), jnp.float32), 'ln2_w': jnp.ones((D,), jnp.float32), 'ln2_b': jnp.zeros((D,), jnp.float32), 'fc_w': jax.random.normal(ks[6], (D, INNER), jnp.float32) * std, 'fc_b': jnp.zeros((INNER,), jnp.float32), 'proj_w': jax.random.normal(ks[7], (INNER, D), jnp.float32) * std, 'proj_b': jnp.zeros((D,), jnp.float32)}
        return inp
    _L0_xattn_all = _L0_xattn_setup()
    _L0_xattn_in = {k: v for k, v in _L0_xattn_all.items() if k in ('ln1_w', 'ln1_b', 'q_w', 'q_b', 'k_w', 'k_b', 'v_w', 'v_b', 'cproj_w', 'cproj_b', 'ln2_w', 'ln2_b', 'fc_w', 'fc_b', 'proj_w', 'proj_b')}
    del _L0_xattn_all
    return {'x': x, 'ctx_2048': ctx_2048, 'mask_BxS2_bf1': mask_BxS2_bf1, 'L0_xattn_ln1_w': _L0_xattn_in['ln1_w'], 'L0_xattn_ln1_b': _L0_xattn_in['ln1_b'], 'L0_xattn_q_w': _L0_xattn_in['q_w'], 'L0_xattn_q_b': _L0_xattn_in['q_b'], 'L0_xattn_k_w': _L0_xattn_in['k_w'], 'L0_xattn_k_b': _L0_xattn_in['k_b'], 'L0_xattn_v_w': _L0_xattn_in['v_w'], 'L0_xattn_v_b': _L0_xattn_in['v_b'], 'L0_xattn_cproj_w': _L0_xattn_in['cproj_w'], 'L0_xattn_cproj_b': _L0_xattn_in['cproj_b'], 'L0_xattn_ln2_w': _L0_xattn_in['ln2_w'], 'L0_xattn_ln2_b': _L0_xattn_in['ln2_b'], 'L0_xattn_fc_w': _L0_xattn_in['fc_w'], 'L0_xattn_fc_b': _L0_xattn_in['fc_b'], 'L0_xattn_proj_w': _L0_xattn_in['proj_w'], 'L0_xattn_proj_b': _L0_xattn_in['proj_b']}

def reference(x, ctx_2048, mask_BxS2_bf1, L0_xattn_ln1_w, L0_xattn_ln1_b, L0_xattn_q_w, L0_xattn_q_b, L0_xattn_k_w, L0_xattn_k_b, L0_xattn_v_w, L0_xattn_v_b, L0_xattn_cproj_w, L0_xattn_cproj_b, L0_xattn_ln2_w, L0_xattn_ln2_b, L0_xattn_fc_w, L0_xattn_fc_b, L0_xattn_proj_w, L0_xattn_proj_b):
    import jax
    import jax.numpy as jnp

    def _L0_xattn_ref(hidden_states, encoder_hidden_states, encoder_attention_mask, ln1_w, ln1_b, q_w, q_b, k_w, k_b, v_w, v_b, cproj_w, cproj_b, ln2_w, ln2_b, fc_w, fc_b, proj_w, proj_b):
        import jax, jax.numpy as jnp
        import numpy as np
        D = 256
        H = 16
        HD = D // H
        INNER = 4 * D
        EPS = 1e-05

        def layer_norm(x, w, b):
            mu = jnp.mean(x, axis=-1, keepdims=True)
            var = jnp.mean(jnp.square(x - mu), axis=-1, keepdims=True)
            return (x - mu) * jax.lax.rsqrt(var + EPS) * w + b
        B, LQ, _ = hidden_states.shape
        LK = encoder_hidden_states.shape[1]
        residual = hidden_states
        x = layer_norm(hidden_states, ln1_w, ln1_b)
        q = (x @ q_w + q_b).reshape(B, LQ, H, HD).transpose(0, 2, 1, 3)
        k = (encoder_hidden_states @ k_w + k_b).reshape(B, LK, H, HD).transpose(0, 2, 1, 3)
        v = (encoder_hidden_states @ v_w + v_b).reshape(B, LK, H, HD).transpose(0, 2, 1, 3)
        scale = 1.0 / np.sqrt(HD).astype(np.float32)
        scores = jnp.einsum('bhqd,bhkd->bhqk', q, k) * scale
        mask = encoder_attention_mask[:, None, None, :]
        mask_value = jnp.finfo(scores.dtype).min
        scores = jnp.where(mask, scores, mask_value)
        attn = jax.nn.softmax(scores, axis=-1)
        out = jnp.einsum('bhqk,bhkd->bhqd', attn, v)
        out = out.transpose(0, 2, 1, 3).reshape(B, LQ, D)
        out = out @ cproj_w + cproj_b
        hidden = out + residual
        residual = hidden
        y = layer_norm(hidden, ln2_w, ln2_b)
        y = jax.nn.gelu(y @ fc_w + fc_b, approximate=True)
        y = y @ proj_w + proj_b
        return residual + y
    x = _L0_xattn_ref(x, ctx_2048, mask_BxS2_bf1, L0_xattn_ln1_w, L0_xattn_ln1_b, L0_xattn_q_w, L0_xattn_q_b, L0_xattn_k_w, L0_xattn_k_b, L0_xattn_v_w, L0_xattn_v_b, L0_xattn_cproj_w, L0_xattn_cproj_b, L0_xattn_ln2_w, L0_xattn_ln2_b, L0_xattn_fc_w, L0_xattn_fc_b, L0_xattn_proj_w, L0_xattn_proj_b)
    return x

_drawn_inputs = setup_inputs


def setup_inputs(seed=0):
    import zlib

    import numpy as np

    out = dict(_drawn_inputs(seed))
    spreads = {'L0_xattn_ln1_w': (1.0, 0.6),
     'L0_xattn_ln1_b': (0.0, 0.8),
     'L0_xattn_q_b': (0.0, 0.8),
     'L0_xattn_k_b': (0.0, 0.8),
     'L0_xattn_v_b': (0.0, 0.1),
     'L0_xattn_cproj_b': (0.0, 0.1),
     'L0_xattn_ln2_w': (1.0, 0.6),
     'L0_xattn_ln2_b': (0.0, 0.734),
     'L0_xattn_fc_b': (0.0, 0.1),
     'L0_xattn_proj_b': (0.0, 0.1)}
    factors = {'L0_xattn_q_w': 8.0, 'L0_xattn_k_w': 8.0}
    for name, (base, spread) in spreads.items():
        noise = np.random.default_rng([zlib.crc32(name.encode()), seed]).standard_normal(out[name].shape)
        drawn = base * np.exp(spread * noise) if base else spread * noise
        out[name] = jnp.asarray(drawn.astype(out[name].dtype))
    for name, factor in factors.items():
        out[name] = (out[name] * factor).astype(out[name].dtype)
    return out
```

```python
from contextlib import ExitStack

import numpy as np

import concourse.bass as bass
from concourse import mybir

F32 = mybir.dt.float32
F32R = mybir.dt.float32r
BF16 = mybir.dt.bfloat16
U8 = mybir.dt.uint8
ALU = mybir.AluOpType
ACT = mybir.ActivationFunctionType
AX = mybir.AxisListType

P = 128
B, S, D, H = 32, 64, 256, 16
HD = D // H
INNER = 4 * D
N = B * S
KC = D // P
MB = INNER // P
GT = 256
TT = GT // P
G = N // GT
BG = GT // S
HP = H // 2
EPS = 1e-5
SCALE = 1.0 / float(np.sqrt(np.float32(HD)))
MASKED = -(2.0 ** 100)
PARTS = 3
Q_SLOTS = (0, 0, 0, 1, 1, 2)
K_SLOTS = (0, 1, 2, 0, 1, 0)
MASK_ROW = HD * len(Q_SLOTS)
LOADS_Q = len(Q_SLOTS)
LOADS_K = len(K_SLOTS) + 1
FC_CHUNKS = MB // 2
LOOPED = True

COLS = {"ln1_w": 0, "ln1_b": 2, "q_b": 4, "k_b": 6, "v_b": 8, "ln2_w": 10, "ln2_b": 12, "fc_b": 14}
N_COLS = 14 + MB


def head_pos(h):
    return (h % 8) * 2 + h // 8


class Group:

    def __init__(self, j, c):
        self.j, self.c = j, c
        self.slot = c % 2

    def count(self, per_group, k=0):
        const = per_group * self.c + k
        if isinstance(self.j, int):
            return 2 * per_group * self.j + const
        return self.j * (2 * per_group) + const

    def loads(self, per_load, before=0):
        const = per_load * (self.c // 2 + 1 - before)
        if isinstance(self.j, int):
            return per_load * self.j + const
        return self.j * per_load + const

    def start(self):
        return self.count(GT)


def wait(eng, sem, value):
    if isinstance(value, int) and value <= 0:
        return
    eng.wait_ge(sem, value)


def build(nc, x, ctx_t, mask, cols, cproj_b, proj_b, q_w, k_w, v_w, cproj_w, fc_w, proj_w, out):
    x_v = x.rearrange("(g t p) d -> g p t d", p=P, t=TT)
    ctx_v = ctx_t.rearrange("(k p) n -> p k n", p=P)
    x_rows = x.rearrange("(t p) d -> p t d", p=P)
    out_rows = out.rearrange("(t p) d -> p t d", p=P)

    with ExitStack() as stack:
        def sb(name, shape, dt=F32):
            return stack.enter_context(nc.sbuf_tensor(name, shape, dt))

        def psum(name, shape, dt=F32):
            return stack.enter_context(nc.psum_tensor(name, shape, dt))

        def sem(name):
            return stack.enter_context(nc.semaphore(name))

        names = ("q", "k", "v", "c")
        w_raw = {n: sb(f"w_raw_{n}", [P, KC, D]) for n in names}
        w_hi = {n: sb(f"w_hi_{n}", [P, KC, D], F32R) for n in names}
        w_lo = {n: sb(f"w_lo_{n}", [P, KC, D], F32R) for n in names}
        fc_raw = sb("fc_raw", [P, KC, INNER])
        fc_hi = sb("fc_hi", [P, KC, INNER], F32R)
        fc_lo = sb("fc_lo", [P, KC, INNER], F32R)
        proj_raw = sb("proj_raw", [P, MB, D])
        proj_hi = sb("proj_hi", [P, MB, D], F32R)
        proj_lo = sb("proj_lo", [P, MB, D], F32R)
        col = sb("col", [P, N_COLS])
        q_bias = sb("q_bias", [P, KC])
        fc_bias = sb("fc_bias", [P, MB])
        vb_rep = sb("vb_rep", [P, KC, P])
        c_bias = sb("c_bias", [P, D])
        cb_rows = sb("cb_rows", [P, D])
        pb_rows = sb("pb_rows", [P, D])

        ident = sb("ident", [P, P])
        ident_b = sb("ident_b", [P, P], BF16)
        select = sb("select", [PARTS * H, HP, 2, S], BF16)
        ones_bd = sb("ones_bd", [P, 2, HD])
        wait_carrier = sb("wait_carrier", [1, 1])
        power = sb("power", [P, TT])
        mask_u8 = sb("mask_u8", [1, N], U8)
        mask_row = sb("mask_row", [1, N], BF16)

        x_in = [sb(f"x_in{s}", [P, TT, D]) for s in range(2)]
        ctx_in = [sb(f"ctx_in{s}", [P, KC, GT]) for s in range(2)]
        ctx_hi = sb("ctx_hi", [P, KC, GT], F32R)
        ctx_lo = sb("ctx_lo", [P, KC, GT], F32R)
        st1 = sb("st1", [P, TT, 6])
        mv1 = sb("mv1", [P, TT, 2])
        ve1 = sb("ve1", [P, TT])
        rs1 = sb("rs1", [P, TT])
        z = sb("z", [P, TT, D])
        z_hi = sb("z_hi", [P, KC, GT], F32R)
        z_lo = sb("z_lo", [P, KC, GT], F32R)
        part = {(n, k): sb(f"part_{n}{k}", [P, KC, GT], BF16) for n in "qk" for k in range(PARTS)}
        rest = {n: sb(f"rest_{n}", [P, KC, GT]) for n in "qk"}
        q_stack = [sb(f"q_stack{s}", [P, H, GT], BF16) for s in range(2)]
        k_stack = [sb(f"k_stack{s}", [P, H, GT], BF16) for s in range(2)]
        v_bd = [sb(f"v_bd{s}", [P, BG, HP, 2, HD]) for s in range(2)]
        xb = [sb(f"xb{s}", [P, TT, D]) for s in range(2)]

        mx = sb("mx", [P, H])
        n_rest = sb("n_rest", [P, H])
        n_parts = sb("n_parts", [P, PARTS, H], BF16)
        n_t = sb("n_t", [PARTS * H, P], BF16)
        probs = [sb(f"probs{p}", [P, HP, 2, S]) for p in range(TT)]
        recip = sb("recip", [P, KC, P])
        o = sb("o", [P, KC, P])
        o_hi = sb("o_hi", [P, KC, P], F32R)
        o_lo = sb("o_lo", [P, KC, P], F32R)
        hid = sb("hid", [P, TT, D])
        hb = [sb(f"hb{s}", [P, TT, D]) for s in range(2)]
        st2 = sb("st2", [P, TT, 6])
        mv2 = sb("mv2", [P, TT, 2])
        ve2 = sb("ve2", [P, TT])
        rs2 = sb("rs2", [P, TT])
        z2 = sb("z2", [P, TT, D])

        z2_hi = sb("z2_hi", [P, KC, GT], F32R)
        z2_lo = sb("z2_lo", [P, KC, GT], F32R)
        gelu = fc_raw[:].rearrange("p k (m t) -> p (k m) t", t=GT)
        g_hi = sb("g_hi", [P, MB, GT], F32R)
        g_lo = sb("g_lo", [P, MB, GT], F32R)
        y = [sb(f"y{s}", [P, TT, D]) for s in range(2)]

        bank0 = psum("bank0", [P, 2, 256])
        bank1 = psum("bank1", [P, 2, 256])
        scores = psum("scores", [P, 2, 512])
        bank4 = psum("bank4", [P, 2, 256])
        bank5 = psum("bank5", [P, 2, 256])
        bank6 = psum("bank6", [P, 2, 256])
        bank7 = psum("bank7", [P, 2, KC, P])
        n_t_ps = bank4[0:PARTS * H, 0, 0:P]
        fc_bank = [bank4, bank5, bank4, bank5]

        w_loaded = {n: sem(f"w_loaded_{n}") for n in ("q", "k", "v", "c", "fc", "proj")}
        col_loaded = sem("col_loaded")
        rows_loaded = sem("rows_loaded")
        mask_loaded = sem("mask_loaded")
        x_loaded = [sem(f"x_loaded{s}") for s in range(2)]
        ctx_loaded = [sem(f"ctx_loaded{s}") for s in range(2)]
        q_stacked = [sem(f"q_stacked{s}") for s in range(2)]
        k_stacked = [sem(f"k_stacked{s}") for s in range(2)]
        stored = [sem(f"stored{s}") for s in range(2)]
        consts_zeroed = sem("consts_zeroed")
        consts_ready = sem("consts_ready")
        ones_zeroed = sem("ones_zeroed")
        ones_ready = sem("ones_ready")
        stacks_set = [sem(f"stacks_set{s}") for s in range(2)]
        v_zeroed = sem("v_zeroed")
        mask_ready = sem("mask_ready")
        vb_repeated = sem("vb_repeated")
        w_high = sem("w_high")
        w_split = sem("w_split")
        bias_summed = sem("bias_summed")
        bias_ready = sem("bias_ready")
        k_made = sem("k_made")
        v_made = sem("v_made")
        z_turned = sem("z_turned")
        q_made = sem("q_made")
        scored = sem("scored")
        n_turned = sem("n_turned")
        shifted = sem("shifted")
        weighed = sem("weighed")
        projected = sem("projected")
        z2_turned = sem("z2_turned")
        fc_made = sem("fc_made")
        mlp_made = sem("mlp_made")
        k_lead = sem("k_lead")
        k_second = sem("k_second")
        q_lead = sem("q_lead")
        q_second = sem("q_second")
        v_even_kept = sem("v_even_kept")
        z_high = sem("z_high")
        n_kept = sem("n_kept")
        exped = sem("exped")
        o_high = sem("o_high")
        z2_high = sem("z2_high")
        gelued = sem("gelued")
        maxed = sem("maxed")
        n_lead = sem("n_lead")
        n_left = sem("n_left")
        n_second = sem("n_second")
        n_split = sem("n_split")
        hid_made = sem("hid_made")
        st2_made = sem("st2_made")
        mv2_made = sem("mv2_made")
        var2_made = sem("var2_made")
        z2_made = sem("z2_made")
        st1_made = sem("st1_made")
        mv1_made = sem("mv1_made")
        var1_made = sem("var1_made")
        z_made = sem("z_made")
        k_left = sem("k_left")
        q_left = sem("q_left")
        v_odd_kept = sem("v_odd_kept")
        recip_made = sem("recip_made")
        o_made = sem("o_made")
        z_split = sem("z_split")
        z2_split = sem("z2_split")
        g_high = sem("g_high")
        g_split = sem("g_split")
        y_made = sem("y_made")
        ctx_high = sem("ctx_high")
        ctx_split = sem("ctx_split")
        rs1_made = sem("rs1_made")
        rs2_made = sem("rs2_made")
        xb_made = sem("xb_made")
        hb_made = sem("hb_made")
        k_third = sem("k_third")
        q_third = sem("q_third")
        o_split = sem("o_split")

        block = stack.enter_context(nc.Block())

        def set_stacks(eng, s):
            pair_of_ones = float(np.array([0x3F803F80], np.uint32).view(np.float32)[0])
            for stacks, word in ((k_stack, 0.0), (q_stack, pair_of_ones)):
                eng.memset(stacks[s][MASK_ROW:P, :, :].rearrange("p h t -> p (h t)").bitcast(F32), word) \
                   .then_inc(stacks_set[s], 1)

        def run_steps(eng, step, first=3, last=G - 2):
            step(Group(0, 0), None, None)
            step(Group(0, 1), Group(0, 0), None)
            for i in range(1, first):
                step(Group(0, i + 1), Group(0, i), Group(0, i - 1))
            if LOOPED:
                with eng.Fori(0, (last - first + 1) // 2) as j:
                    for c in range(2):
                        step(Group(j, c + first + 1), Group(j, c + first), Group(j, c + first - 1))
            else:
                for i in range(first, last + 1):
                    step(Group(0, i + 1), Group(0, i), Group(0, i - 1))
            for i in range(last + 1, G + 1):
                step(Group(0, i + 1) if i + 1 < G else None, Group(0, i) if i < G else None, Group(0, i - 1))

        @block.sync
        def _(sp):
            def load(g):
                wait(sp, z_made, g.count(1, -1))
                wait(sp, xb_made, g.count(1, -1))
                sp.dma_start(x_in[g.slot][:], x_rows[:, bass.ds(g.count(TT), TT), :]).then_inc(x_loaded[g.slot], 16)
                wait(sp, ctx_split, g.count(1, -1))
                sp.dma_start(ctx_in[g.slot][:],
                             ctx_v[:, :, bass.ds(g.start(), GT)]).then_inc(ctx_loaded[g.slot], 16)

            def stack_up(g, name, slots, stacks, stacked, third):
                wait(sp, third, g.count(1, 1))
                wait(sp, shifted, g.count(4, -4))
                for n, k in enumerate(slots):
                    sp.dma_start(stacks[g.slot][HD * n:HD * (n + 1), :, :].rearrange("r (h m) t -> r h (m t)", m=KC),
                                 part[name, k][:].rearrange("p m t -> p (m t)")).then_inc(stacked[g.slot], 16)

            def step(a, b, c, ahead=True):
                if a is not None:
                    if a.c < 2 and isinstance(a.j, int):
                        sp.wait_ge(stacks_set[a.slot], 2)
                        sp.wait_ge(mask_ready, 1)
                    wait(sp, shifted, a.count(4, -4))
                    sp.dma_start(k_stack[a.slot][MASK_ROW:MASK_ROW + 1, :, :],
                                 mask_row[0:1, bass.ds(a.start(), GT)].unsqueeze(1).broadcast_to([1, H, GT])) \
                      .then_inc(k_stacked[a.slot], 16)
                    stack_up(a, "k", K_SLOTS, k_stack, k_stacked, k_third)
                    stack_up(a, "q", Q_SLOTS, q_stack, q_stacked, q_third)
                    if ahead:
                        load(Group(a.j, a.c + 1))
                if c is not None:
                    sp.wait_ge(y_made, c.count(1, 1))
                    sp.dma_start(out_rows[:, bass.ds(c.count(TT), TT), :], y[c.slot][:]).then_inc(stored[c.slot], 16)

            load(Group(0, 0))
            sp.dma_start(w_raw["k"][:], k_w.rearrange("(k p) n -> p k n", p=P)).then_inc(w_loaded["k"], 16)
            sp.dma_start(w_raw["v"][:], v_w.rearrange("(k p) n -> p k n", p=P)).then_inc(w_loaded["v"], 16)
            sp.dma_start(col[:], cols[:, :]).then_inc(col_loaded, 16)
            sp.dma_start(w_raw["q"][:], q_w.rearrange("(k p) n -> p k n", p=P)).then_inc(w_loaded["q"], 16)
            sp.dma_start(mask_u8[:], mask.rearrange("(a n) -> a n", a=1)).then_inc(mask_loaded, 16)
            sp.dma_start(w_raw["c"][:], cproj_w.rearrange("(k p) n -> p k n", p=P)).then_inc(w_loaded["c"], 16)
            sp.dma_start(cb_rows[:], cproj_b.rearrange("(a n) -> a n", a=1).broadcast_to([P, D])).then_inc(rows_loaded, 16)
            sp.dma_start(pb_rows[:], proj_b.rearrange("(a n) -> a n", a=1).broadcast_to([P, D])).then_inc(rows_loaded, 16)
            step(Group(0, 0), None, None)
            sp.dma_start(fc_raw[:], fc_w.rearrange("(k p) n -> p k n", p=P)).then_inc(w_loaded["fc"], 16)
            sp.dma_start(proj_raw[:], proj_w.rearrange("(k p) n -> p k n", p=P)).then_inc(w_loaded["proj"], 16)
            step(Group(0, 1), Group(0, 0), None)
            if LOOPED:
                with sp.Fori(0, (G - 4) // 2) as j:
                    for c in range(2):
                        step(Group(j, c + 2), Group(j, c + 1), Group(j, c))
            else:
                for i in range(1, G - 3):
                    step(Group(0, i + 1), Group(0, i), Group(0, i - 1))
            for i in range(G - 3, G + 1):
                step(Group(0, i + 1) if i + 1 < G else None, None, Group(0, i - 1), ahead=i + 2 < G)
            for s in range(2):
                sp.wait_ge(stored[s], 16 * (G // 2))

        @block.gpsimd
        def _(pool):
            gp = nc.gpsimd
            gp.memset(ident[:], 0.0).then_inc(consts_zeroed, 1)
            gp.memset(ident_b[:], 0.0).then_inc(consts_zeroed, 1)
            gp.memset(select[:], 0.0).then_inc(consts_zeroed, 1)
            gp.memset(power[:], -0.5).then_inc(consts_zeroed, 1)
            pool.wait_ge(consts_zeroed, 4)
            for t in (ident, ident_b):
                gp.affine_select(out=t[:], in_=t[:], compare_op=ALU.not_equal, fill=1.0, base=0,
                                 pattern=[[-1, P]], channel_multiplier=1).then_inc(consts_ready, 1)
            for k in range(PARTS):
                if k:
                    pool.wait_ge(consts_ready, 2 + k)
                gp.affine_select(out=select[:], in_=select[:], compare_op=ALU.not_equal, fill=1.0, base=-H * k,
                                 pattern=[[-2, HP], [-1, 2], [0, S]], channel_multiplier=1).then_inc(consts_ready, 1)

            def step(a, b, c):
                if a is not None:
                    pool.wait_ge(ctx_loaded[a.slot], a.loads(16))
                    wait(pool, v_made, a.count(1))
                    pool.wait_ge(ctx_high, a.count(1, 1))
                    gp.tensor_tensor(ctx_lo[:], ctx_in[a.slot][:], ctx_hi[:].bitcast(F32),
                                     ALU.subtract).then_inc(ctx_split, 1)
                    if a.c == 0 and isinstance(a.j, int):
                        for s in range(2):
                            gp.memset(v_bd[s][:], 0.0).then_inc(v_zeroed, 1)
                if a is not None:
                    pool.wait_ge(var1_made, a.count(1, 1))
                    wait(pool, z_made, a.count(1))
                    gp.tensor_tensor(rs1[:], ve1[:], power[:], ALU.pow).then_inc(rs1_made, 1)
                if c is not None:
                    row_scale(c, 1)
                    keep_hidden(c, 1)
                if a is not None:
                    third(a, "k", k_second, k_stacked, 16 * LOADS_K, k_third)
                    pool.wait_ge(x_loaded[a.slot], a.loads(16))
                    if a.c == 0 and isinstance(a.j, int):
                        pool.wait_ge(bias_ready, 2)
                    wait(pool, hid_made, a.count(2, -2))
                    gp.tensor_tensor(xb[a.slot][:], x_in[a.slot][:],
                                     c_bias[:].unsqueeze(1).broadcast_to([P, TT, D]), ALU.add).then_inc(xb_made, 1)
                if b is not None:
                    rest_of_o(b, 0)
                if a is not None:
                    third(a, "q", q_second, q_stacked, 16 * LOADS_Q, q_third)
                if b is not None:
                    rest_of_o(b, 1)
                    row_scale(b, 0)
                    keep_hidden(b, 0)

            def third(g, n, second, stacked, per_load, made):
                pool.wait_ge(second, g.count(1, 1))
                before = Group(g.j, g.c - 1)
                if not (isinstance(g.j, int) and g.c == 0):
                    wait(pool, stacked[before.slot], before.loads(per_load))
                gp.tensor_tensor(part[n, 2][:], rest[n][:], part[n, 1][:], ALU.subtract).then_inc(made, 1)

            def row_scale(g, p):
                pool.wait_ge(var2_made, g.count(2, p + 1))
                gp.tensor_tensor(rs2[:, p:p + 1], ve2[:, p:p + 1], power[:, 0:1], ALU.pow).then_inc(rs2_made, 1)

            def keep_hidden(g, p):
                pool.wait_ge(hid_made, g.count(2, p + 1))
                if p == 0:
                    wait(pool, y_made, g.count(1, -1))
                gp.tensor_tensor(hb[g.slot][:, p, :], hid[:, p, :], pb_rows[:], ALU.add).then_inc(hb_made, 1)

            def rest_of_o(g, p):
                pool.wait_ge(o_high, g.count(2, p + 1))
                wait(pool, projected, g.count(2, p))
                gp.tensor_tensor(o_lo[:], o[:], o_hi[:].bitcast(F32), ALU.subtract).then_inc(o_split, 1)

            run_steps(pool, step)

        @block.scalar
        def _(act):
            sc = nc.scalar
            act.wait_ge(w_loaded["k"], 16)
            sc.copy(w_hi["k"][:], w_raw["k"][:]).then_inc(w_high, 1)
            act.wait_ge(w_loaded["v"], 16)
            sc.copy(w_hi["v"][:], w_raw["v"][:]).then_inc(w_high, 1)
            act.wait_ge(w_loaded["q"], 16)
            act.wait_ge(col_loaded, 16)
            for k in range(KC):
                w1 = col[:, COLS["ln1_w"] + k:COLS["ln1_w"] + k + 1]
                last = sc.activation(w_hi["q"][:, k, :], w_raw["q"][:, k, :], ACT.Copy, scale=w1)
            last.then_inc(w_high, 1)
            act.wait_ge(w_loaded["c"], 16)
            sc.copy(w_hi["c"][:], w_raw["c"][:]).then_inc(w_high, 1)

            def lead(g, n, made, bank, bias, stacked, per_load, first):
                act.wait_ge(made, g.count(1, 1))
                before = Group(g.j, g.c - 1)
                if not (isinstance(g.j, int) and g.c == 0):
                    wait(act, stacked[before.slot], before.loads(per_load))
                for m in range(KC):
                    last = sc.activation(part[n, 0][:, m, :], bank[:, m, :], ACT.Identity, bias=bias[:, m:m + 1])
                last.then_inc(first, 1)

            def second(g, n, left, made):
                act.wait_ge(left, g.count(1, 1))
                sc.copy(part[n, 1][:], rest[n][:]).then_inc(made, 1)

            def keep_maxima(g, p):
                act.wait_ge(n_turned, g.count(2, p + 1))
                wait(act, shifted, g.count(4, 2 * p))
                sc.copy(n_t[:], n_t_ps).then_inc(n_kept, 1)

            def exp(g, p):
                wait(act, weighed, g.count(2, p - 1))
                for s in range(2):
                    act.wait_ge(shifted, g.count(4, 2 * p + s + 1))
                    sc.activation(probs[p][:, 4 * s:4 * s + 4, :, :],
                                  scores[:, s, :].rearrange("p (h b q) -> p h b q", h=4, b=2),
                                  ACT.Exp, scale=SCALE).then_inc(exped, 1)

            def o_lead(g, p):
                act.wait_ge(o_made, g.count(2, p + 1))
                wait(act, projected, g.count(2, p))
                sc.copy(o_hi[:], o[:]).then_inc(o_high, 1)

            def chunk(g, m):
                act.wait_ge(fc_made, g.count(4, m + 1))
                for h in range(2):
                    last = sc.activation(gelu[:, 2 * m + h, :], fc_bank[m][:, h, :], ACT.Gelu_apprx_tanh,
                                         bias=fc_bias[:, 2 * m + h:2 * m + h + 1])
                last.then_inc(gelued, 1)

            def step(a, b, c):
                if a is not None:
                    act.wait_ge(ctx_loaded[a.slot], a.loads(16))
                    wait(act, v_made, a.count(1))
                    sc.copy(ctx_hi[:], ctx_in[a.slot][:]).then_inc(ctx_high, 1)
                    lead(a, "k", k_made, bank0, col[:, COLS["k_b"]:COLS["k_b"] + KC], k_stacked, 16 * LOADS_K, k_lead)
                if b is not None:
                    keep_maxima(b, 0)
                if a is not None:
                    second(a, "k", k_left, k_second)
                if b is not None:
                    exp(b, 0)
                if a is not None:
                    act.wait_ge(v_made, a.count(1, 1))
                    if a.c < 2 and isinstance(a.j, int):
                        act.wait_ge(v_zeroed, 2)
                    wait(act, weighed, a.count(2, -2))
                    for par in range(2):
                        last = sc.copy(
                            v_bd[a.slot][S * par:S * par + S, :, :, par, :]
                            .rearrange("p (t b) h d -> p t b h d", b=2)[:, :, 0, :, :],
                            bank6[0:S, :, :].rearrange("p t (h w d) -> p t h w d", w=2, d=HD)[:, :, :, par, :])
                    last.then_inc(v_even_kept, 1)
                    act.wait_ge(z_turned, a.count(1, 1))
                    wait(act, q_made, a.count(1))
                    sc.copy(z_hi[:], bank1[:]).then_inc(z_high, 1)
                if b is not None:
                    keep_maxima(b, 1)
                if c is not None:
                    act.wait_ge(z2_turned, c.count(1, 1))
                    wait(act, fc_made, c.count(4))
                    sc.copy(z2_hi[:], bank0[:]).then_inc(z2_high, 1)
                if b is not None:
                    exp(b, 1)
                if a is not None:
                    if a.c == 0 and isinstance(a.j, int):
                        act.wait_ge(bias_ready, 1)
                    lead(a, "q", q_made, bank1, q_bias, q_stacked, 16 * LOADS_Q, q_lead)
                    second(a, "q", q_left, q_second)
                if b is not None:
                    o_lead(b, 0)
                if c is not None:
                    if c.c == 0 and isinstance(c.j, int):
                        act.wait_ge(bias_ready, 3)
                    chunk(c, 0)
                    chunk(c, 1)
                if b is not None:
                    o_lead(b, 1)
                if c is not None:
                    chunk(c, 2)
                    chunk(c, 3)
                if a is not None and a.c == 0 and isinstance(a.j, int):
                    act.wait_ge(w_loaded["fc"], 16)
                    for k in range(KC):
                        w2 = col[:, COLS["ln2_w"] + k:COLS["ln2_w"] + k + 1]
                        sc.activation(fc_hi[:, k, :], fc_raw[:, k, :], ACT.Copy, scale=w2).then_inc(w_high, 1)
                    act.wait_ge(w_loaded["proj"], 16)
                    sc.copy(proj_hi[:], proj_raw[:]).then_inc(w_high, 1)

            run_steps(act, step)

        @block.vector
        def _(dve):
            ve = nc.vector
            for n, name in enumerate(("k", "v")):
                dve.wait_ge(w_high, n + 1)
                ve.tensor_tensor(w_lo[name][:], w_raw[name][:], w_hi[name][:].bitcast(F32),
                                 ALU.subtract).then_inc(w_split, 1)
            dve.wait_ge(mask_loaded, 16)
            ve.tensor_scalar(mask_row[:], mask_u8[:], 1.0, -MASKED, ALU.subtract, ALU.mult).then_inc(mask_ready, 1)
            dve.wait_ge(col_loaded, 16)
            ve.tensor_copy(vb_rep[:], col[:, COLS["v_b"]:COLS["v_b"] + KC].unsqueeze(2).broadcast_to([P, KC, P])) \
              .then_inc(vb_repeated, 1)
            ve.memset(ones_bd[:], 0.0).then_inc(ones_zeroed, 1)
            dve.wait_ge(ones_zeroed, 1)
            for w in range(2):
                ve.memset(ones_bd[S * w:S * w + S, w, :], 1.0).then_inc(ones_ready, 1)
            set_stacks(ve, 0)
            dve.wait_ge(w_high, 3)
            for k in range(KC):
                w1 = col[:, COLS["ln1_w"] + k:COLS["ln1_w"] + k + 1]
                last = ve.scalar_tensor_tensor(w_lo["q"][:, k, :], w_raw["q"][:, k, :], w1,
                                               w_hi["q"][:, k, :].bitcast(F32), ALU.mult, ALU.subtract)
            last.then_inc(w_split, 1)
            dve.wait_ge(w_high, 4)
            ve.tensor_tensor(w_lo["c"][:], w_raw["c"][:], w_hi["c"][:].bitcast(F32), ALU.subtract).then_inc(w_split, 1)

            def carry_wait():
                ve.memset(wait_carrier[:], 0.0)

            def maxima(g, p):
                dve.wait_ge(scored, g.count(2, p + 1))
                ve.reduce_max(mx[:], scores[:, :, :].rearrange("p s (h k) -> p (s h) k", k=S),
                              AX.X).then_inc(maxed, 1)
                dve.wait_ge(maxed, g.count(2, p + 1))
                wait(dve, n_turned, g.count(2, p))
                ve.tensor_scalar(n_parts[:, 0, :], mx[:], -1.0, None, ALU.mult).then_inc(n_lead, 1)
                dve.wait_ge(n_lead, g.count(2, p + 1))
                ve.scalar_tensor_tensor(n_rest[:], mx[:], -1.0, n_parts[:, 0, :],
                                        ALU.mult, ALU.subtract).then_inc(n_left, 1)
                dve.wait_ge(n_left, g.count(2, p + 1))
                ve.tensor_copy(n_parts[:, 1, :], n_rest[:]).then_inc(n_second, 1)
                dve.wait_ge(n_second, g.count(2, p + 1))
                ve.tensor_tensor(n_parts[:, 2, :], n_rest[:], n_parts[:, 1, :], ALU.subtract).then_inc(n_split, 1)

            def hidden(g, p):
                bank = (bank1, bank5)[p]
                dve.wait_ge(projected, g.count(2, p + 1))
                dve.wait_ge(xb_made, g.count(1, 1))
                wait(dve, hb_made, g.count(2, p - 1))
                ve.tensor_tensor(hid[:, p, :], bank[:, 0, :], xb[g.slot][:, p, :], ALU.add).then_inc(hid_made, 1)
                dve.wait_ge(hid_made, g.count(2, p + 1))
                ve.bn_stats(st2[:, p, :], hid[:, p, :]).then_inc(st2_made, 1)
                dve.wait_ge(st2_made, g.count(2, p + 1))
                carry_wait()
                ve.bn_aggr(mv2[:, p, :], st2[:, p, :]).then_inc(mv2_made, 1)
                dve.wait_ge(mv2_made, g.count(2, p + 1))
                ve.tensor_scalar(ve2[:, p:p + 1], mv2[:, p, 1:2], EPS, None, ALU.add).then_inc(var2_made, 1)

            def normal2(g, p):
                dve.wait_ge(rs2_made, g.count(2, p + 1))
                wait(dve, z2_turned, g.count(1))
                ve.tensor_scalar(z2[:, p, :], hid[:, p, :], mv2[:, p, 0:1], rs2[:, p:p + 1],
                                 ALU.subtract, ALU.mult).then_inc(z2_made, 1)

            def left(g, n, lead, bank, bias, second, rest_made):
                dve.wait_ge(lead, g.count(1, 1))
                wait(dve, second, g.count(1))
                for m in range(KC):
                    last = ve.scalar_tensor_tensor(rest[n][:, m, :], bank[:, m, :], bias[:, m:m + 1],
                                                   part[n, 0][:, m, :], ALU.add, ALU.subtract)
                last.then_inc(rest_made, 1)

            def outputs(g, p):
                dve.wait_ge(weighed, g.count(2, p + 1))
                ve.reciprocal(recip[:], bank7[:, 1, :, :]).then_inc(recip_made, 1)
                dve.wait_ge(recip_made, g.count(2, p + 1))
                wait(dve, o_split, g.count(2, p))
                ve.tensor_tensor(o[:], bank7[:, 0, :, :], recip[:], ALU.mult).then_inc(o_made, 1)

            def parts_of(g, m):
                dve.wait_ge(gelued, g.count(4, m + 1))
                wait(dve, mlp_made, g.count(1))
                ve.tensor_copy(g_hi[:, 2 * m:2 * m + 2, :], gelu[:, 2 * m:2 * m + 2, :]).then_inc(g_high, 1)
                dve.wait_ge(g_high, g.count(4, m + 1))
                ve.tensor_tensor(g_lo[:, 2 * m:2 * m + 2, :], gelu[:, 2 * m:2 * m + 2, :],
                                 g_hi[:, 2 * m:2 * m + 2, :].bitcast(F32), ALU.subtract).then_inc(g_split, 1)

            def step(a, b, c):
                if b is not None:
                    maxima(b, 0)
                if a is not None:
                    dve.wait_ge(x_loaded[a.slot], a.loads(16))
                    for t in range(TT):
                        last = ve.bn_stats(st1[:, t, :], x_in[a.slot][:, t, :])
                    last.then_inc(st1_made, 1)
                    dve.wait_ge(st1_made, a.count(1, 1))
                    carry_wait()
                    for t in range(TT):
                        last = ve.bn_aggr(mv1[:, t, :], st1[:, t, :])
                    last.then_inc(mv1_made, 1)
                    dve.wait_ge(mv1_made, a.count(1, 1))
                    ve.tensor_scalar(ve1[:], mv1[:, :, 1], EPS, None, ALU.add).then_inc(var1_made, 1)
                if c is not None:
                    hidden(c, 1)
                if a is not None:
                    dve.wait_ge(rs1_made, a.count(1, 1))
                    wait(dve, z_turned, a.count(1))
                    for t in range(TT):
                        last = ve.tensor_scalar(z[:, t, :], x_in[a.slot][:, t, :], mv1[:, t, 0:1], rs1[:, t:t + 1],
                                                ALU.subtract, ALU.mult)
                    last.then_inc(z_made, 1)
                if c is not None:
                    normal2(c, 1)
                if a is not None:
                    left(a, "k", k_lead, bank0, col[:, COLS["k_b"]:COLS["k_b"] + KC], k_third, k_left)
                    if a.c == 0 and isinstance(a.j, int):
                        dve.wait_ge(bias_summed, 1)
                        ve.tensor_tensor(q_bias[:], bank7[:, 0, 0, 0:KC], col[:, COLS["q_b"]:COLS["q_b"] + KC],
                                         ALU.add).then_inc(bias_ready, 1)
                        dve.wait_ge(bias_summed, 2)
                        dve.wait_ge(rows_loaded, 32)
                        ve.tensor_tensor(c_bias[:], bank5[:, 0, :], cb_rows[:], ALU.add).then_inc(bias_ready, 1)
                    dve.wait_ge(v_made, a.count(1, 1))
                    wait(dve, weighed, a.count(2, -2))
                    for par in range(2):
                        last = ve.tensor_copy(
                            v_bd[a.slot][S * par:S * par + S, :, :, par, :]
                            .rearrange("p (t b) h d -> p t b h d", b=2)[:, :, 1, :, :],
                            bank6[S:P, :, :].rearrange("p t (h w d) -> p t h w d", w=2, d=HD)[:, :, :, par, :])
                    last.then_inc(v_odd_kept, 1)
                if b is not None:
                    maxima(b, 1)
                    outputs(b, 0)
                if a is not None:
                    dve.wait_ge(z_high, a.count(1, 1))
                    wait(dve, q_made, a.count(1))
                    ve.tensor_tensor(z_lo[:], bank1[:], z_hi[:].bitcast(F32), ALU.subtract).then_inc(z_split, 1)
                if c is not None:
                    dve.wait_ge(z2_high, c.count(1, 1))
                    wait(dve, fc_made, c.count(4))
                    ve.tensor_tensor(z2_lo[:], bank0[:], z2_hi[:].bitcast(F32), ALU.subtract).then_inc(z2_split, 1)
                if a is not None:
                    left(a, "q", q_lead, bank1, q_bias, q_third, q_left)
                if c is not None:
                    parts_of(c, 0)
                    parts_of(c, 1)
                if b is not None:
                    outputs(b, 1)
                if c is not None:
                    parts_of(c, 2)
                    parts_of(c, 3)
                if b is not None:
                    hidden(b, 0)
                    normal2(b, 0)
                if c is not None:
                    dve.wait_ge(mlp_made, c.count(1, 1))
                    dve.wait_ge(hb_made, c.count(2, 2))
                    wait(dve, stored[c.slot], c.loads(16, before=1))
                    ve.tensor_tensor(y[c.slot][:], bank6[:], hb[c.slot][:], ALU.add).then_inc(y_made, 1)
                if a is not None and a.c == 0 and isinstance(a.j, int):
                    set_stacks(ve, 1)
                    for k in range(KC):
                        w2 = col[:, COLS["ln2_w"] + k:COLS["ln2_w"] + k + 1]
                        dve.wait_ge(w_high, 5 + k)
                        ve.scalar_tensor_tensor(fc_lo[:, k, :], fc_raw[:, k, :], w2, fc_hi[:, k, :].bitcast(F32),
                                                ALU.mult, ALU.subtract).then_inc(w_split, 1)
                    dve.wait_ge(w_high, 7)
                    ve.tensor_tensor(proj_lo[:], proj_raw[:], proj_hi[:].bitcast(F32),
                                     ALU.subtract).then_inc(w_split, 1)
                    dve.wait_ge(bias_summed, 3)
                    ve.tensor_tensor(fc_bias[:], bank5[:, 1, 0:MB], col[:, COLS["fc_b"]:COLS["fc_b"] + MB],
                                     ALU.add).then_inc(bias_ready, 1)

            run_steps(dve, step)

        @block.tensor
        def _(pe):
            mm = nc.tensor.matmul

            def three_pass(out_ap, a_hi, a_lo, b_hi, b_lo, first, last):
                mm(out_ap, a_hi, b_hi, start=first, stop=False, skip_group_check=True)
                mm(out_ap, a_lo, b_hi, start=False, stop=False, skip_group_check=True)
                return mm(out_ap, a_hi, b_lo, start=False, stop=last, skip_group_check=True)

            def by_feature(bank, name, r_hi, r_lo):
                for m in range(KC):
                    cols_m = slice(P * m, P * m + P)
                    for k in range(KC):
                        last = three_pass(bank[:, m, :], w_hi[name][:, k, cols_m], w_lo[name][:, k, cols_m],
                                          r_hi[:, k, :], r_lo[:, k, :], m == 0 and k == 0, k == KC - 1)
                return last

            def turn(bank, src):
                for t in range(TT):
                    for k in range(KC):
                        last = nc.tensor.transpose(bank[:, k, P * t:P * t + P], src[:, t, P * k:P * k + P], ident[:])
                return last

            def score(g, p):
                wait(pe, exped, g.count(4, 2 * p))
                q, k = q_stack[g.slot], k_stack[g.slot]
                for h in range(H):
                    for b in range(2):
                        rows = slice(S * (2 * p + b), S * (2 * p + b) + S)
                        last = mm(scores[S * b:S * b + S, h // 8, S * (h % 8):S * (h % 8) + S],
                                  q[:, head_pos(h), rows], k[:, head_pos(h), rows], start=True, stop=True,
                                  skip_group_check=True)
                last.then_inc(scored, 1)

            def turn_maxima(g, p):
                pe.wait_ge(n_split, g.count(2, p + 1))
                mm(n_t_ps, n_parts[:].rearrange("p k h -> p (k h)"), ident_b[:], start=True, stop=True,
                   skip_group_check=True).then_inc(n_turned, 1)

            def shift(g, p):
                q, k = q_stack[g.slot], k_stack[g.slot]
                pe.wait_ge(n_kept, g.count(2, p + 1))
                for s in range(2):
                    for i in range(4):
                        mm(scores[:, s, P * i:P * i + P], select[:, 4 * s + i, :, :].rearrange("r w k -> r (w k)"),
                           n_t[:], start=(i == 0), stop=False, skip_group_check=True)
                    for i in range(4):
                        for b in range(2):
                            rows = slice(S * (2 * p + b), S * (2 * p + b) + S)
                            for par in range(2):
                                pos = head_pos(2 * (4 * s + i) + par)
                                last = mm(scores[S * par:S * par + S, s, P * i + S * b:P * i + S * b + S],
                                          k[:, pos, rows], q[:, pos, rows], start=False, stop=True,
                                          skip_group_check=True)
                    last.then_inc(shifted, 1)

            def weigh(g, p):
                pe.wait_ge(exped, g.count(4, 2 * p + 2))
                wait(pe, o_made, g.count(2, p))
                for half in range(KC):
                    for b in range(2):
                        cols_b = slice(S * b, S * b + S)
                        for kind in range(2):
                            for i in range(4):
                                hp = 4 * half + i
                                w = ones_bd[:] if kind else v_bd[g.slot][:, 2 * p + b, hp, :, :]
                                last = mm(bank7[32 * i:32 * i + 32, kind, half, cols_b],
                                          w.rearrange("p w d -> p (w d)"), probs[p][:, hp, b, :],
                                          start=True, stop=True, skip_group_check=True)
                last.then_inc(weighed, 1)

            def project(g, p):
                pe.wait_ge(o_split, g.count(2, p + 1))
                if p == 0:
                    if g_next := nexts[0]:
                        pe.wait_ge(q_left, g_next.count(1, 1))
                    bank = bank1
                else:
                    bank = bank5
                for k in range(KC):
                    last = three_pass(bank[:, 0, :], o_hi[:, k, :], o_lo[:, k, :], w_hi["c"][:, k, :],
                                      w_lo["c"][:, k, :], k == 0, k == KC - 1)
                last.then_inc(projected, 1)

            def fc_chunk(g, m):
                bank = fc_bank[m]
                for h in range(2):
                    cols_m = slice(P * (2 * m + h), P * (2 * m + h) + P)
                    for k in range(KC):
                        last = three_pass(bank[:, h, :], fc_hi[:, k, cols_m], fc_lo[:, k, cols_m],
                                          z2_hi[:, k, :], z2_lo[:, k, :], h == 0 and k == 0, k == KC - 1)
                last.then_inc(fc_made, 1)

            nexts = [None]

            def step(a, b, c):
                nexts[0] = a
                if b is not None:
                    pe.wait_ge(k_stacked[b.slot], b.loads(16 * LOADS_K))
                    pe.wait_ge(q_stacked[b.slot], b.loads(16 * LOADS_Q))
                    score(b, 0)
                if c is not None:
                    project(c, 1)
                if a is not None:
                    if a.c == 0 and isinstance(a.j, int):
                        pe.wait_ge(w_split, 2)
                    pe.wait_ge(ctx_split, a.count(1, 1))
                    wait(pe, z2_split, a.count(1, -2))
                    by_feature(bank0, "k", ctx_hi, ctx_lo).then_inc(k_made, 1)
                    wait(pe, y_made, a.count(1, -2))
                    for t in range(TT):
                        rows = slice(P * t, P * t + P)
                        for k in range(KC):
                            last = three_pass(bank6[:, t, :], ctx_hi[:, k, rows], ctx_lo[:, k, rows],
                                              w_hi["v"][:, k, :], w_lo["v"][:, k, :], t == 0 and k == 0, k == KC - 1)
                    last.then_inc(v_made, 1)
                if b is not None:
                    turn_maxima(b, 0)
                    shift(b, 0)
                if a is not None:
                    if a.c == 0 and isinstance(a.j, int):
                        pe.wait_ge(consts_ready, 2 + PARTS)
                        pe.wait_ge(ones_ready, 2)
                        pe.wait_ge(col_loaded, 16)
                        pe.wait_ge(w_loaded["q"], 16)
                        for m in range(KC):
                            for k in range(KC):
                                b1 = col[:, COLS["ln1_b"] + k:COLS["ln1_b"] + k + 1]
                                last = mm(bank7[:, 0, 0, m:m + 1], w_raw["q"][:, k, P * m:P * m + P], b1,
                                          start=(m == 0 and k == 0), stop=(k == KC - 1), skip_group_check=True)
                        last.then_inc(bias_summed, 1)
                        pe.wait_ge(w_loaded["c"], 16)
                        pe.wait_ge(vb_repeated, 1)
                        for k in range(KC):
                            last = mm(bank5[:, 0, :], vb_rep[:, k, :], w_raw["c"][:, k, :], start=(k == 0),
                                      stop=(k == KC - 1), skip_group_check=True)
                        last.then_inc(bias_summed, 1)
                    pe.wait_ge(z_made, a.count(1, 1))
                    wait(pe, hid_made, a.count(2, -3))
                    turn(bank1, z).then_inc(z_turned, 1)
                if b is not None:
                    score(b, 1)
                    if b.c == 0 and isinstance(b.j, int):
                        pe.wait_ge(v_even_kept, 1)
                        pe.wait_ge(v_odd_kept, 1)
                    weigh(b, 0)
                if c is not None:
                    pe.wait_ge(z2_made, c.count(2, 2))
                    if a is not None:
                        pe.wait_ge(k_left, a.count(1, 1))
                    turn(bank0, z2).then_inc(z2_turned, 1)
                if b is not None:
                    turn_maxima(b, 1)
                    shift(b, 1)
                if a is not None:
                    if a.c == 0 and isinstance(a.j, int):
                        pe.wait_ge(w_split, 4)
                    pe.wait_ge(z_split, a.count(1, 1))
                    by_feature(bank1, "q", z_hi, z_lo).then_inc(q_made, 1)
                if c is not None:
                    pe.wait_ge(z2_split, c.count(1, 1))
                    if c.c == 0 and isinstance(c.j, int):
                        pe.wait_ge(w_split, 7)
                        pe.wait_ge(bias_ready, 3)
                    fc_chunk(c, 0)
                    pe.wait_ge(hid_made, c.count(2, 2))
                    fc_chunk(c, 1)
                if b is not None:
                    weigh(b, 1)
                if c is not None:
                    for m in (2, 3):
                        pe.wait_ge(gelued, c.count(4, m - 1))
                        fc_chunk(c, m)
                if b is not None:
                    project(b, 0)
                if c is not None:
                    if a is not None:
                        pe.wait_ge(v_even_kept, a.count(1, 1))
                        pe.wait_ge(v_odd_kept, a.count(1, 1))
                    else:
                        wait(pe, y_made, c.count(1))
                    for m in range(FC_CHUNKS):
                        pe.wait_ge(g_split, c.count(4, m + 1))
                        for t in range(TT):
                            rows = slice(P * t, P * t + P)
                            for k in (2 * m, 2 * m + 1):
                                last = three_pass(bank6[:, t, :], g_hi[:, k, rows], g_lo[:, k, rows],
                                                  proj_hi[:, k, :], proj_lo[:, k, :], k == 0 and t == 0, k == MB - 1)
                    last.then_inc(mlp_made, 1)
                if a is not None and a.c == 0 and isinstance(a.j, int):
                    pe.wait_ge(w_loaded["fc"], 16)
                    pe.wait_ge(bias_ready, 2)
                    for m in range(MB):
                        for k in range(KC):
                            b2 = col[:, COLS["ln2_b"] + k:COLS["ln2_b"] + k + 1]
                            last = mm(bank5[:, 1, m:m + 1], fc_raw[:, k, P * m:P * m + P], b2,
                                      start=(m == 0 and k == 0), stop=(k == KC - 1), skip_group_check=True)
                    last.then_inc(bias_summed, 1)

            run_steps(pe, step)


_INS = ("x", "ctx_t", "mask", "cols", "cproj_b", "proj_b", "q_w", "k_w", "v_w", "cproj_w", "fc_w", "proj_w")


def kernel(**inputs):
    import concourse.bacc as bacc
    from concourse.bass_utils import run_bass_kernel_spmd

    def by_partition(name):
        return np.asarray(inputs["L0_xattn_" + name]).reshape(-1, P).T

    def head_minor(w):
        halves = w.reshape(*w.shape[:-1], KC, P // HD, HD)
        return np.swapaxes(halves, -1, -2).reshape(w.shape)

    inputs = dict(inputs)
    for n in ("q_w", "q_b", "k_w", "k_b"):
        inputs["L0_xattn_" + n] = head_minor(np.asarray(inputs["L0_xattn_" + n]))
    arrays = {
        "x": np.asarray(inputs["x"]).reshape(N, D),
        "ctx_t": np.asarray(inputs["ctx_2048"]).reshape(N, D).T,
        "mask": np.asarray(inputs["mask_BxS2_bf1"]).reshape(N).view(np.uint8),
        "cols": np.concatenate([by_partition(n) for n in COLS], axis=1),
    }
    for n in _INS[4:]:
        arrays[n] = np.asarray(inputs["L0_xattn_" + n])
    arrays = {n: np.ascontiguousarray(arrays[n]) for n in _INS}

    nc = bacc.Bacc("TRN2", target_bir_lowering=False, num_devices=1)
    args = [nc.dram_tensor(f"in_{n}", a.shape, mybir.dt.from_np(a.dtype), kind="ExternalInput").ap()
            for n, a in arrays.items()]
    out = nc.dram_tensor("out", (N, D), F32, kind="ExternalOutput").ap()
    build(nc, *args, out)
    r = run_bass_kernel_spmd(nc, [{f"in_{n}": a for n, a in arrays.items()}], core_ids=[0])
    return r.results[0]["out"].reshape(B, S, D)
```

```python
from contextlib import ExitStack

import numpy as np

import concourse.bass as bass
from concourse import mybir

F32 = mybir.dt.float32
F32R = mybir.dt.float32r
BF16 = mybir.dt.bfloat16
U8 = mybir.dt.uint8
ALU = mybir.AluOpType
ACT = mybir.ActivationFunctionType
AX = mybir.AxisListType

P = 128
B, S, D, H = 32, 64, 256, 16
HD = D // H
INNER = 4 * D
N = B * S
KC = D // P
MB = INNER // P
GT = 256
TT = GT // P
G = N // GT
BG = GT // S
HP = H // 2
EPS = 1e-5
SCALE = 1.0 / float(np.sqrt(np.float32(HD)))
MASKED = -(2.0 ** 100)
PARTS = 3
Q_SLOTS = (0, 0, 0, 1, 1, 2)
K_SLOTS = (0, 1, 2, 0, 1, 0)
MASK_ROW = HD * len(Q_SLOTS)
LOADS_Q = len(Q_SLOTS)
LOADS_K = len(K_SLOTS) + 1
FC_CHUNKS = MB // 2
LOOPED = True

COLS = {"ln1_w": 0, "ln1_b": 2, "q_b": 4, "k_b": 6, "v_b": 8, "ln2_w": 10, "ln2_b": 12, "fc_b": 14}
N_COLS = 14 + MB


def head_pos(h):
    return (h % 8) * 2 + h // 8


class Group:

    def __init__(self, j, c):
        self.j, self.c = j, c
        self.slot = c % 2

    def count(self, per_group, k=0):
        const = per_group * self.c + k
        if isinstance(self.j, int):
            return 2 * per_group * self.j + const
        return self.j * (2 * per_group) + const

    def loads(self, per_load, before=0):
        const = per_load * (self.c // 2 + 1 - before)
        if isinstance(self.j, int):
            return per_load * self.j + const
        return self.j * per_load + const

    def start(self):
        return self.count(GT)


def wait(eng, sem, value):
    if isinstance(value, int) and value <= 0:
        return
    eng.wait_ge(sem, value)


def build(nc, x, ctx_t, mask, cols, cproj_b, proj_b, q_w, k_w, v_w, cproj_w, fc_w, proj_w, out):
    x_v = x.rearrange("(g t p) d -> g p t d", p=P, t=TT)
    ctx_v = ctx_t.rearrange("(k p) n -> p k n", p=P)
    x_rows = x.rearrange("(t p) d -> p t d", p=P)
    out_rows = out.rearrange("(t p) d -> p t d", p=P)

    with ExitStack() as stack:
        def sb(name, shape, dt=F32):
            return stack.enter_context(nc.sbuf_tensor(name, shape, dt))

        def psum(name, shape, dt=F32):
            return stack.enter_context(nc.psum_tensor(name, shape, dt))

        def sem(name):
            return stack.enter_context(nc.semaphore(name))

        names = ("q", "k", "v", "c")
        w_raw = {n: sb(f"w_raw_{n}", [P, KC, D]) for n in names}
        w_hi = {n: sb(f"w_hi_{n}", [P, KC, D], F32R) for n in names}
        w_lo = {n: sb(f"w_lo_{n}", [P, KC, D], F32R) for n in names}
        fc_raw = sb("fc_raw", [P, KC, INNER])
        fc_hi = sb("fc_hi", [P, KC, INNER], F32R)
        fc_lo = sb("fc_lo", [P, KC, INNER], F32R)
        proj_raw = sb("proj_raw", [P, MB, D])
        proj_hi = sb("proj_hi", [P, MB, D], F32R)
        proj_lo = sb("proj_lo", [P, MB, D], F32R)
        col = sb("col", [P, N_COLS])
        q_bias = sb("q_bias", [P, KC])
        fc_bias = sb("fc_bias", [P, MB])
        vb_rep = sb("vb_rep", [P, KC, P])
        c_bias = sb("c_bias", [P, D])
        cb_rows = sb("cb_rows", [P, D])
        pb_rows = sb("pb_rows", [P, D])

        ident = sb("ident", [P, P])
        ident_b = sb("ident_b", [P, P], BF16)
        select = sb("select", [PARTS * H, HP, 2, S], BF16)
        ones_bd = sb("ones_bd", [P, 2, HD])
        wait_carrier = sb("wait_carrier", [1, 1])
        table_scratch = sb("table_scratch", [1, 1])
        power = sb("power", [P, TT])
        mask_u8 = sb("mask_u8", [1, N], U8)
        mask_row = sb("mask_row", [1, N], BF16)

        x_in = [sb(f"x_in{s}", [P, TT, D]) for s in range(2)]
        ctx_in = [sb(f"ctx_in{s}", [P, KC, GT]) for s in range(2)]
        ctx_hi = sb("ctx_hi", [P, KC, GT], F32R)
        ctx_lo = sb("ctx_lo", [P, KC, GT], F32R)
        st1 = sb("st1", [P, TT, 6])
        mv1 = sb("mv1", [P, TT, 2])
        ve1 = sb("ve1", [P, TT])
        rs1 = sb("rs1", [P, TT])
        z = sb("z", [P, TT, D])
        z_hi = sb("z_hi", [P, KC, GT], F32R)
        z_lo = sb("z_lo", [P, KC, GT], F32R)
        part = {(n, k): sb(f"part_{n}{k}", [P, KC, GT], BF16) for n in "qk" for k in range(PARTS)}
        rest = {n: sb(f"rest_{n}", [P, KC, GT]) for n in "qk"}
        q_stack = [sb(f"q_stack{s}", [P, H, GT], BF16) for s in range(2)]
        k_stack = [sb(f"k_stack{s}", [P, H, GT], BF16) for s in range(2)]
        v_bd = [sb(f"v_bd{s}", [P, BG, HP, 2, HD]) for s in range(2)]
        xb = [sb(f"xb{s}", [P, TT, D]) for s in range(2)]

        mx = sb("mx", [P, H])
        n_rest = sb("n_rest", [P, H])
        n_parts = sb("n_parts", [P, PARTS, H], BF16)
        n_t = sb("n_t", [PARTS * H, P], BF16)
        probs = [sb(f"probs{p}", [P, HP, 2, S]) for p in range(TT)]
        recip = sb("recip", [P, KC, P])
        o = sb("o", [P, KC, P])
        o_hi = sb("o_hi", [P, KC, P], F32R)
        o_lo = sb("o_lo", [P, KC, P], F32R)
        hid = sb("hid", [P, TT, D])
        hb = [sb(f"hb{s}", [P, TT, D]) for s in range(2)]
        st2 = sb("st2", [P, TT, 6])
        mv2 = sb("mv2", [P, TT, 2])
        ve2 = sb("ve2", [P, TT])
        rs2 = sb("rs2", [P, TT])
        z2 = sb("z2", [P, TT, D])

        z2_hi = sb("z2_hi", [P, KC, GT], F32R)
        z2_lo = sb("z2_lo", [P, KC, GT], F32R)
        gelu = fc_raw[:].rearrange("p k (m t) -> p (k m) t", t=GT)
        g_hi = sb("g_hi", [P, MB, GT], F32R)
        g_lo = sb("g_lo", [P, MB, GT], F32R)
        y = [sb(f"y{s}", [P, TT, D]) for s in range(2)]

        bank0 = psum("bank0", [P, 2, 256])
        bank1 = psum("bank1", [P, 2, 256])
        scores = psum("scores", [P, 2, 512])
        bank4 = psum("bank4", [P, 2, 256])
        bank5 = psum("bank5", [P, 2, 256])
        bank6 = psum("bank6", [P, 2, 256])
        bank7 = psum("bank7", [P, 2, KC, P])
        n_t_ps = bank4[0:PARTS * H, 0, 0:P]
        fc_bank = [bank4, bank5, bank4, bank5]

        w_loaded = {n: sem(f"w_loaded_{n}") for n in ("q", "k", "v", "c", "fc", "proj")}
        col_loaded = sem("col_loaded")
        rows_loaded = sem("rows_loaded")
        mask_loaded = sem("mask_loaded")
        x_loaded = [sem(f"x_loaded{s}") for s in range(2)]
        ctx_loaded = [sem(f"ctx_loaded{s}") for s in range(2)]
        q_stacked = [sem(f"q_stacked{s}") for s in range(2)]
        k_stacked = [sem(f"k_stacked{s}") for s in range(2)]
        stored = [sem(f"stored{s}") for s in range(2)]
        idents_zeroed = sem("idents_zeroed")
        idents_ready = sem("idents_ready")
        select_set = sem("select_set")
        ones_zeroed = sem("ones_zeroed")
        ones_ready = sem("ones_ready")
        stacks_set = [sem(f"stacks_set{s}") for s in range(2)]
        v_zeroed = sem("v_zeroed")
        mask_ready = sem("mask_ready")
        vb_repeated = sem("vb_repeated")
        w_high = sem("w_high")
        w_split = sem("w_split")
        bias_summed = sem("bias_summed")
        bias_ready = sem("bias_ready")
        k_made = sem("k_made")
        v_made = sem("v_made")
        z_turned = sem("z_turned")
        q_made = sem("q_made")
        scored = sem("scored")
        n_turned = sem("n_turned")
        shifted = sem("shifted")
        weighed = sem("weighed")
        projected = sem("projected")
        z2_turned = sem("z2_turned")
        fc_made = sem("fc_made")
        mlp_made = sem("mlp_made")
        k_lead = sem("k_lead")
        k_second = sem("k_second")
        q_lead = sem("q_lead")
        q_second = sem("q_second")
        v_even_kept = sem("v_even_kept")
        z_high = sem("z_high")
        n_kept = sem("n_kept")
        exped = sem("exped")
        o_high = sem("o_high")
        z2_high = sem("z2_high")
        gelued = sem("gelued")
        maxed = sem("maxed")
        n_lead = sem("n_lead")
        n_left = sem("n_left")
        n_second = sem("n_second")
        n_split = sem("n_split")
        hid_made = sem("hid_made")
        st2_made = sem("st2_made")
        mv2_made = sem("mv2_made")
        var2_made = sem("var2_made")
        z2_made = sem("z2_made")
        st1_made = sem("st1_made")
        mv1_made = sem("mv1_made")
        var1_made = sem("var1_made")
        z_made = sem("z_made")
        k_left = sem("k_left")
        q_left = sem("q_left")
        v_odd_kept = sem("v_odd_kept")
        recip_made = sem("recip_made")
        o_made = sem("o_made")
        z_split = sem("z_split")
        z2_split = sem("z2_split")
        g_high = sem("g_high")
        g_split = sem("g_split")
        y_made = sem("y_made")
        ctx_high = sem("ctx_high")
        ctx_split = sem("ctx_split")
        rs1_made = sem("rs1_made")
        rs2_made = sem("rs2_made")
        xb_made = sem("xb_made")
        hb_made = sem("hb_made")
        k_third = sem("k_third")
        q_third = sem("q_third")
        o_split = sem("o_split")

        block = stack.enter_context(nc.Block())

        def set_stacks(eng, s):
            pair_of_ones = float(np.array([0x3F803F80], np.uint32).view(np.float32)[0])
            for stacks, word in ((k_stack, 0.0), (q_stack, pair_of_ones)):
                eng.memset(stacks[s][MASK_ROW:P, :, :].rearrange("p h t -> p (h t)").bitcast(F32), word) \
                   .then_inc(stacks_set[s], 1)

        def run_steps(eng, first_step, step, first=3, last=G - 2):
            first_step(Group(0, 0))
            step(Group(0, 1), Group(0, 0), None)
            for i in range(1, first):
                step(Group(0, i + 1), Group(0, i), Group(0, i - 1))
            if LOOPED:
                with eng.Fori(0, (last - first + 1) // 2) as j:
                    for c in range(2):
                        step(Group(j, c + first + 1), Group(j, c + first), Group(j, c + first - 1))
            else:
                for i in range(first, last + 1):
                    step(Group(0, i + 1), Group(0, i), Group(0, i - 1))
            for i in range(last + 1, G + 1):
                step(Group(0, i + 1) if i + 1 < G else None, Group(0, i) if i < G else None, Group(0, i - 1))

        @block.sync
        def _(sp):
            def stack_up(g, name, slots, stacks, stacked, made):
                for k in range(PARTS):
                    sp.wait_ge(made[k], g.count(1, 1))
                    for n in range(len(slots)):
                        if slots[n] == k:
                            sp.dma_start(stacks[g.slot][HD * n:HD * (n + 1), :, :]
                                         .rearrange("r (h m) t -> r h (m t)", m=KC),
                                         part[name, k][:].rearrange("p m t -> p (m t)")) \
                              .then_inc(stacked[g.slot], 16)

            def stack_mask(g):
                sp.dma_start(k_stack[g.slot][MASK_ROW:MASK_ROW + 1, :, :],
                             mask_row[0:1, bass.ds(g.start(), GT)].unsqueeze(1).broadcast_to([1, H, GT])) \
                  .then_inc(k_stacked[g.slot], 16)

            def stack_k(g):
                stack_up(g, "k", K_SLOTS, k_stack, k_stacked, (k_lead, k_second, k_third))

            def stack_q(g):
                stack_up(g, "q", Q_SLOTS, q_stack, q_stacked, (q_lead, q_second, q_third))

            def first_step(a):
                stack_k(a)
                sp.wait_ge(stacks_set[0], 2)
                sp.wait_ge(mask_ready, 1)
                stack_mask(a)
                stack_q(a)

            def step(a, b, c, ahead=True):
                if a is not None:
                    if c is None:
                        sp.wait_ge(stacks_set[1], 2)
                    wait(sp, shifted, a.count(4, -4))
                    stack_mask(a)
                    stack_k(a)
                    stack_q(a)
                    if ahead:
                        load_x(Group(a.j, a.c + 1))
                        load_ctx(Group(a.j, a.c + 1))
                if c is not None:
                    sp.wait_ge(y_made, c.count(1, 1))
                    sp.dma_start(out_rows[:, bass.ds(c.count(TT), TT), :], y[c.slot][:]).then_inc(stored[c.slot], 16)

            def load_x(g):
                wait(sp, z_made, g.count(1, -1))
                wait(sp, xb_made, g.count(1, -1))
                sp.dma_start(x_in[g.slot][:], x_rows[:, bass.ds(g.count(TT), TT), :]).then_inc(x_loaded[g.slot], 16)

            def load_ctx(g):
                wait(sp, ctx_split, g.count(1, -1))
                sp.dma_start(ctx_in[g.slot][:],
                             ctx_v[:, :, bass.ds(g.start(), GT)]).then_inc(ctx_loaded[g.slot], 16)

            def load_w(name, dst, w):
                sp.dma_start(dst[:], w.rearrange("(k p) n -> p k n", p=P)).then_inc(w_loaded[name], 16)

            load_ctx(Group(0, 0))
            load_w("k", w_raw["k"], k_w)
            load_x(Group(0, 0))
            load_w("v", w_raw["v"], v_w)
            sp.dma_start(col[:], cols[:, :]).then_inc(col_loaded, 16)
            load_w("q", w_raw["q"], q_w)
            sp.dma_start(mask_u8[:], mask.rearrange("(a n) -> a n", a=1)).then_inc(mask_loaded, 16)
            load_w("c", w_raw["c"], cproj_w)
            sp.dma_start(cb_rows[:], cproj_b.rearrange("(a n) -> a n", a=1).broadcast_to([P, D])).then_inc(rows_loaded, 16)
            load_w("fc", fc_raw, fc_w)
            sp.dma_start(pb_rows[:], proj_b.rearrange("(a n) -> a n", a=1).broadcast_to([P, D])).then_inc(rows_loaded, 16)
            load_ctx(Group(0, 1))
            load_x(Group(0, 1))
            load_w("proj", proj_raw, proj_w)
            first_step(Group(0, 0))
            step(Group(0, 1), Group(0, 0), None)
            if LOOPED:
                with sp.Fori(0, (G - 4) // 2) as j:
                    for c in range(2):
                        step(Group(j, c + 2), Group(j, c + 1), Group(j, c))
            else:
                for i in range(1, G - 3):
                    step(Group(0, i + 1), Group(0, i), Group(0, i - 1))
            for i in range(G - 3, G + 1):
                step(Group(0, i + 1) if i + 1 < G else None, None, Group(0, i - 1), ahead=i + 2 < G)
            for s in range(2):
                sp.wait_ge(stored[s], 16 * (G // 2))

        @block.gpsimd
        def _(pool):
            gp = nc.gpsimd
            gp.memset(ident[:], 0.0).then_inc(idents_zeroed, 1)
            gp.memset(ident_b[:], 0.0).then_inc(idents_zeroed, 1)
            gp.memset(power[:], -0.5)
            pool.wait_ge(idents_zeroed, 2)
            for t in (ident, ident_b):
                gp.affine_select(out=t[:], in_=t[:], compare_op=ALU.not_equal, fill=1.0, base=0,
                                 pattern=[[-1, P]], channel_multiplier=1).then_inc(idents_ready, 1)

            def set_select():
                gp.memset(select[:], 0.0).then_inc(select_set, 1)
                for k in range(PARTS):
                    pool.wait_ge(select_set, 1 + k)
                    gp.affine_select(out=select[:], in_=select[:], compare_op=ALU.not_equal, fill=1.0, base=-H * k,
                                     pattern=[[-2, HP], [-1, 2], [0, S]], channel_multiplier=1) \
                      .then_inc(select_set, 1)

            def rest_of_ctx(a):
                pool.wait_ge(ctx_loaded[a.slot], a.loads(16))
                wait(pool, v_made, a.count(1))
                pool.wait_ge(ctx_high, a.count(1, 1))
                gp.tensor_tensor(ctx_lo[:], ctx_in[a.slot][:], ctx_hi[:].bitcast(F32),
                                 ALU.subtract).then_inc(ctx_split, 1)

            def scale_1(a):
                pool.wait_ge(var1_made, a.count(1, 1))
                wait(pool, z_made, a.count(1))
                gp.tensor_tensor(rs1[:], ve1[:], power[:], ALU.pow).then_inc(rs1_made, 1)

            def x_and_bias(a):
                pool.wait_ge(x_loaded[a.slot], a.loads(16))
                wait(pool, hid_made, a.count(2, -2))
                gp.tensor_tensor(xb[a.slot][:], x_in[a.slot][:],
                                 c_bias[:].unsqueeze(1).broadcast_to([P, TT, D]), ALU.add).then_inc(xb_made, 1)

            def first_step(a):
                rest_of_ctx(a)
                pool.wait_ge(idents_ready, 2)
                scale_1(a)
                for s in range(2):
                    gp.memset(v_bd[s][:], 0.0).then_inc(v_zeroed, 1)
                third(a, "k", k_second, k_stacked, 16 * LOADS_K, k_third)
                pool.wait_ge(bias_ready, 2)
                x_and_bias(a)
                third(a, "q", q_second, q_stacked, 16 * LOADS_Q, q_third)
                set_select()

            def step(a, b, c):
                if a is not None:
                    rest_of_ctx(a)
                    scale_1(a)
                if c is not None:
                    row_scale(c, 1)
                    keep_hidden(c, 1)
                if a is not None:
                    third(a, "k", k_second, k_stacked, 16 * LOADS_K, k_third)
                    x_and_bias(a)
                if b is not None:
                    rest_of_o(b, 0)
                if a is not None:
                    third(a, "q", q_second, q_stacked, 16 * LOADS_Q, q_third)
                if b is not None:
                    rest_of_o(b, 1)
                    row_scale(b, 0)
                    keep_hidden(b, 0)

            def third(g, n, second, stacked, per_load, made):
                pool.wait_ge(second, g.count(1, 1))
                before = Group(g.j, g.c - 1)
                if not (isinstance(g.j, int) and g.c == 0):
                    wait(pool, stacked[before.slot], before.loads(per_load))
                gp.tensor_tensor(part[n, 2][:], rest[n][:], part[n, 1][:], ALU.subtract).then_inc(made, 1)

            def row_scale(g, p):
                pool.wait_ge(var2_made, g.count(2, p + 1))
                gp.tensor_tensor(rs2[:, p:p + 1], ve2[:, p:p + 1], power[:, 0:1], ALU.pow).then_inc(rs2_made, 1)

            def keep_hidden(g, p):
                pool.wait_ge(hid_made, g.count(2, p + 1))
                if p == 0:
                    wait(pool, y_made, g.count(1, -1))
                gp.tensor_tensor(hb[g.slot][:, p, :], hid[:, p, :], pb_rows[:], ALU.add).then_inc(hb_made, 1)

            def rest_of_o(g, p):
                pool.wait_ge(o_high, g.count(2, p + 1))
                wait(pool, projected, g.count(2, p))
                gp.tensor_tensor(o_lo[:], o[:], o_hi[:].bitcast(F32), ALU.subtract).then_inc(o_split, 1)

            run_steps(pool, first_step, step)

        @block.scalar
        def _(act):
            sc = nc.scalar
            def fetch_table(func):
                sc.activation(table_scratch[:], power[0:1, 0:1], func)

            def lead(g, n, made, bank, bias, stacked, per_load, first):
                act.wait_ge(made, g.count(1, 1))
                before = Group(g.j, g.c - 1)
                if not (isinstance(g.j, int) and g.c == 0):
                    wait(act, stacked[before.slot], before.loads(per_load))
                for m in range(KC):
                    last = sc.activation(part[n, 0][:, m, :], bank[:, m, :], ACT.Identity, bias=bias[:, m:m + 1])
                last.then_inc(first, 1)

            def second(g, n, left, made):
                act.wait_ge(left, g.count(1, 1))
                sc.copy(part[n, 1][:], rest[n][:]).then_inc(made, 1)

            def keep_maxima(g, p):
                act.wait_ge(n_turned, g.count(2, p + 1))
                wait(act, shifted, g.count(4, 2 * p))
                sc.copy(n_t[:], n_t_ps).then_inc(n_kept, 1)

            def exp(g, p):
                wait(act, weighed, g.count(2, p - 1))
                for s in range(2):
                    act.wait_ge(shifted, g.count(4, 2 * p + s + 1))
                    sc.activation(probs[p][:, 4 * s:4 * s + 4, :, :],
                                  scores[:, s, :].rearrange("p (h b q) -> p h b q", h=4, b=2),
                                  ACT.Exp, scale=SCALE).then_inc(exped, 1)

            def o_lead(g, p):
                act.wait_ge(o_made, g.count(2, p + 1))
                wait(act, projected, g.count(2, p))
                sc.copy(o_hi[:], o[:]).then_inc(o_high, 1)

            def chunk(g, m):
                act.wait_ge(fc_made, g.count(4, m + 1))
                for h in range(2):
                    last = sc.activation(gelu[:, 2 * m + h, :], fc_bank[m][:, h, :], ACT.Gelu_apprx_tanh,
                                         bias=fc_bias[:, 2 * m + h:2 * m + h + 1])
                last.then_inc(gelued, 1)

            def high(dst, src, count):
                sc.copy(dst[:], src[:]).then_inc(count, 1)

            def high_of_ctx(a):
                act.wait_ge(ctx_loaded[a.slot], a.loads(16))
                wait(act, v_made, a.count(1))
                high(ctx_hi, ctx_in[a.slot], ctx_high)

            def keep_even_v(a, zeroed=False):
                act.wait_ge(v_made, a.count(1, 1))
                if zeroed:
                    act.wait_ge(v_zeroed, 2)
                wait(act, weighed, a.count(2, -2))
                for par in range(2):
                    last = sc.copy(
                        v_bd[a.slot][S * par:S * par + S, :, :, par, :]
                        .rearrange("p (t b) h d -> p t b h d", b=2)[:, :, 0, :, :],
                        bank6[0:S, :, :].rearrange("p t (h w d) -> p t h w d", w=2, d=HD)[:, :, :, par, :])
                last.then_inc(v_even_kept, 1)

            def high_of_z(a):
                act.wait_ge(z_turned, a.count(1, 1))
                wait(act, q_made, a.count(1))
                high(z_hi, bank1, z_high)

            def lead_k(a):
                lead(a, "k", k_made, bank0, col[:, COLS["k_b"]:COLS["k_b"] + KC], k_stacked, 16 * LOADS_K, k_lead)

            def lead_q(a):
                lead(a, "q", q_made, bank1, q_bias, q_stacked, 16 * LOADS_Q, q_lead)

            def first_step(a):
                act.wait_ge(w_loaded["k"], 16)
                high(w_hi["k"], w_raw["k"], w_high)
                high_of_ctx(a)
                act.wait_ge(w_loaded["v"], 16)
                high(w_hi["v"], w_raw["v"], w_high)
                act.wait_ge(w_loaded["q"], 16)
                act.wait_ge(col_loaded, 16)
                for k in range(KC):
                    w1 = col[:, COLS["ln1_w"] + k:COLS["ln1_w"] + k + 1]
                    last = sc.activation(w_hi["q"][:, k, :], w_raw["q"][:, k, :], ACT.Copy, scale=w1)
                last.then_inc(w_high, 1)
                lead_k(a)
                high_of_z(a)
                second(a, "k", k_left, k_second)
                keep_even_v(a, zeroed=True)
                act.wait_ge(bias_ready, 1)
                lead_q(a)
                second(a, "q", q_left, q_second)
                act.wait_ge(w_loaded["c"], 16)
                high(w_hi["c"], w_raw["c"], w_high)
                act.wait_ge(w_loaded["fc"], 16)
                for k in range(KC):
                    w2 = col[:, COLS["ln2_w"] + k:COLS["ln2_w"] + k + 1]
                    sc.activation(fc_hi[:, k, :], fc_raw[:, k, :], ACT.Copy, scale=w2).then_inc(w_high, 1)
                act.wait_ge(idents_ready, 2)

            def step(a, b, c):
                if a is not None:
                    high_of_ctx(a)
                if b is not None:
                    fetch_table(ACT.Exp)
                if a is not None:
                    lead_k(a)
                if b is not None:
                    keep_maxima(b, 0)
                if b is not None:
                    exp(b, 0)
                if a is not None:
                    second(a, "k", k_left, k_second)
                if a is not None:
                    keep_even_v(a, zeroed=c is None)
                    high_of_z(a)
                if b is not None:
                    keep_maxima(b, 1)
                if c is not None:
                    act.wait_ge(z2_turned, c.count(1, 1))
                    wait(act, fc_made, c.count(4))
                    high(z2_hi, bank0, z2_high)
                if b is not None:
                    exp(b, 1)
                if c is not None:
                    fetch_table(ACT.Gelu_apprx_tanh)
                if a is not None:
                    lead_q(a)
                    second(a, "q", q_left, q_second)
                if b is not None:
                    o_lead(b, 0)
                if c is not None:
                    if c.c == 0 and isinstance(c.j, int):
                        act.wait_ge(bias_ready, 3)
                    chunk(c, 0)
                    chunk(c, 1)
                    chunk(c, 2)
                if b is not None:
                    o_lead(b, 1)
                if c is not None:
                    chunk(c, 3)
                if b is not None and c is None:
                    act.wait_ge(w_loaded["proj"], 16)
                    high(proj_hi, proj_raw, w_high)

            run_steps(act, first_step, step)

        @block.vector
        def _(dve):
            ve = nc.vector
            def rest_of_w(name, count):
                dve.wait_ge(w_high, count)
                ve.tensor_tensor(w_lo[name][:], w_raw[name][:], w_hi[name][:].bitcast(F32),
                                 ALU.subtract).then_inc(w_split, 1)
            def carry_wait():
                ve.memset(wait_carrier[:], 0.0)

            def maxima(g, p):
                dve.wait_ge(scored, g.count(2, p + 1))
                ve.reduce_max(mx[:], scores[:, :, :].rearrange("p s (h k) -> p (s h) k", k=S),
                              AX.X).then_inc(maxed, 1)
                dve.wait_ge(maxed, g.count(2, p + 1))
                wait(dve, n_turned, g.count(2, p))
                ve.tensor_scalar(n_parts[:, 0, :], mx[:], -1.0, None, ALU.mult).then_inc(n_lead, 1)
                dve.wait_ge(n_lead, g.count(2, p + 1))
                ve.scalar_tensor_tensor(n_rest[:], mx[:], -1.0, n_parts[:, 0, :],
                                        ALU.mult, ALU.subtract).then_inc(n_left, 1)
                dve.wait_ge(n_left, g.count(2, p + 1))
                ve.tensor_copy(n_parts[:, 1, :], n_rest[:]).then_inc(n_second, 1)
                dve.wait_ge(n_second, g.count(2, p + 1))
                ve.tensor_tensor(n_parts[:, 2, :], n_rest[:], n_parts[:, 1, :], ALU.subtract).then_inc(n_split, 1)

            def hidden(g, p):
                bank = (bank1, bank5)[p]
                dve.wait_ge(projected, g.count(2, p + 1))
                dve.wait_ge(xb_made, g.count(1, 1))
                wait(dve, hb_made, g.count(2, p - 1))
                ve.tensor_tensor(hid[:, p, :], bank[:, 0, :], xb[g.slot][:, p, :], ALU.add).then_inc(hid_made, 1)
                dve.wait_ge(hid_made, g.count(2, p + 1))
                ve.bn_stats(st2[:, p, :], hid[:, p, :]).then_inc(st2_made, 1)
                dve.wait_ge(st2_made, g.count(2, p + 1))
                carry_wait()
                ve.bn_aggr(mv2[:, p, :], st2[:, p, :]).then_inc(mv2_made, 1)
                dve.wait_ge(mv2_made, g.count(2, p + 1))
                ve.tensor_scalar(ve2[:, p:p + 1], mv2[:, p, 1:2], EPS, None, ALU.add).then_inc(var2_made, 1)

            def normal2(g, p):
                dve.wait_ge(rs2_made, g.count(2, p + 1))
                wait(dve, z2_turned, g.count(1))
                ve.tensor_scalar(z2[:, p, :], hid[:, p, :], mv2[:, p, 0:1], rs2[:, p:p + 1],
                                 ALU.subtract, ALU.mult).then_inc(z2_made, 1)

            def left(g, n, lead, bank, bias, second, rest_made):
                dve.wait_ge(lead, g.count(1, 1))
                wait(dve, second, g.count(1))
                for m in range(KC):
                    last = ve.scalar_tensor_tensor(rest[n][:, m, :], bank[:, m, :], bias[:, m:m + 1],
                                                   part[n, 0][:, m, :], ALU.add, ALU.subtract)
                last.then_inc(rest_made, 1)

            def outputs(g, p):
                dve.wait_ge(weighed, g.count(2, p + 1))
                ve.reciprocal(recip[:], bank7[:, 1, :, :]).then_inc(recip_made, 1)
                dve.wait_ge(recip_made, g.count(2, p + 1))
                wait(dve, o_split, g.count(2, p))
                ve.tensor_tensor(o[:], bank7[:, 0, :, :], recip[:], ALU.mult).then_inc(o_made, 1)

            def parts_of(g, m):
                dve.wait_ge(gelued, g.count(4, m + 1))
                wait(dve, mlp_made, g.count(1))
                ve.tensor_copy(g_hi[:, 2 * m:2 * m + 2, :], gelu[:, 2 * m:2 * m + 2, :]).then_inc(g_high, 1)
                dve.wait_ge(g_high, g.count(4, m + 1))
                ve.tensor_tensor(g_lo[:, 2 * m:2 * m + 2, :], gelu[:, 2 * m:2 * m + 2, :],
                                 g_hi[:, 2 * m:2 * m + 2, :].bitcast(F32), ALU.subtract).then_inc(g_split, 1)

            def normal1_stats(a):
                dve.wait_ge(x_loaded[a.slot], a.loads(16))
                for t in range(TT):
                    last = ve.bn_stats(st1[:, t, :], x_in[a.slot][:, t, :])
                last.then_inc(st1_made, 1)
                dve.wait_ge(st1_made, a.count(1, 1))
                carry_wait()
                for t in range(TT):
                    last = ve.bn_aggr(mv1[:, t, :], st1[:, t, :])
                last.then_inc(mv1_made, 1)
                dve.wait_ge(mv1_made, a.count(1, 1))
                ve.tensor_scalar(ve1[:], mv1[:, :, 1], EPS, None, ALU.add).then_inc(var1_made, 1)

            def normal1(a):
                dve.wait_ge(rs1_made, a.count(1, 1))
                wait(dve, z_turned, a.count(1))
                for t in range(TT):
                    last = ve.tensor_scalar(z[:, t, :], x_in[a.slot][:, t, :], mv1[:, t, 0:1], rs1[:, t:t + 1],
                                            ALU.subtract, ALU.mult)
                last.then_inc(z_made, 1)

            def left_k(a):
                left(a, "k", k_lead, bank0, col[:, COLS["k_b"]:COLS["k_b"] + KC], k_third, k_left)

            def left_q(a):
                left(a, "q", q_lead, bank1, q_bias, q_third, q_left)

            def keep_odd_v(a):
                dve.wait_ge(v_made, a.count(1, 1))
                wait(dve, weighed, a.count(2, -2))
                for par in range(2):
                    last = ve.tensor_copy(
                        v_bd[a.slot][S * par:S * par + S, :, :, par, :]
                        .rearrange("p (t b) h d -> p t b h d", b=2)[:, :, 1, :, :],
                        bank6[S:P, :, :].rearrange("p t (h w d) -> p t h w d", w=2, d=HD)[:, :, :, par, :])
                last.then_inc(v_odd_kept, 1)

            def rest_of_z(a):
                dve.wait_ge(z_high, a.count(1, 1))
                wait(dve, q_made, a.count(1))
                ve.tensor_tensor(z_lo[:], bank1[:], z_hi[:].bitcast(F32), ALU.subtract).then_inc(z_split, 1)

            def first_step(a):
                rest_of_w("k", 1)
                normal1_stats(a)
                rest_of_w("v", 2)
                dve.wait_ge(col_loaded, 16)
                ve.tensor_copy(vb_rep[:], col[:, COLS["v_b"]:COLS["v_b"] + KC].unsqueeze(2)
                               .broadcast_to([P, KC, P])).then_inc(vb_repeated, 1)
                ve.memset(ones_bd[:], 0.0).then_inc(ones_zeroed, 1)
                dve.wait_ge(ones_zeroed, 1)
                for w in range(2):
                    ve.memset(ones_bd[S * w:S * w + S, w, :], 1.0).then_inc(ones_ready, 1)
                normal1(a)
                dve.wait_ge(w_high, 3)
                for k in range(KC):
                    w1 = col[:, COLS["ln1_w"] + k:COLS["ln1_w"] + k + 1]
                    last = ve.scalar_tensor_tensor(w_lo["q"][:, k, :], w_raw["q"][:, k, :], w1,
                                                   w_hi["q"][:, k, :].bitcast(F32), ALU.mult, ALU.subtract)
                last.then_inc(w_split, 1)
                left_k(a)
                rest_of_z(a)
                dve.wait_ge(mask_loaded, 16)
                ve.tensor_scalar(mask_row[:], mask_u8[:], 1.0, -MASKED, ALU.subtract,
                                 ALU.mult).then_inc(mask_ready, 1)
                dve.wait_ge(v_zeroed, 2)
                keep_odd_v(a)
                dve.wait_ge(bias_summed, 1)
                ve.tensor_tensor(q_bias[:], bank7[:, 0, 0, 0:KC], col[:, COLS["q_b"]:COLS["q_b"] + KC],
                                 ALU.add).then_inc(bias_ready, 1)
                dve.wait_ge(bias_summed, 2)
                dve.wait_ge(rows_loaded, 32)
                ve.tensor_tensor(c_bias[:], bank5[:, 0, :], cb_rows[:], ALU.add).then_inc(bias_ready, 1)
                left_q(a)
                set_stacks(ve, 0)
                rest_of_w("c", 4)
                for k in range(KC):
                    w2 = col[:, COLS["ln2_w"] + k:COLS["ln2_w"] + k + 1]
                    dve.wait_ge(w_high, 5 + k)
                    ve.scalar_tensor_tensor(fc_lo[:, k, :], fc_raw[:, k, :], w2, fc_hi[:, k, :].bitcast(F32),
                                            ALU.mult, ALU.subtract).then_inc(w_split, 1)
                dve.wait_ge(bias_summed, 3)
                ve.tensor_tensor(fc_bias[:], bank5[:, 1, 0:MB], col[:, COLS["fc_b"]:COLS["fc_b"] + MB],
                                 ALU.add).then_inc(bias_ready, 1)

            def step(a, b, c):
                if b is not None and c is None:
                    normal1_stats(a)
                    set_stacks(ve, 1)
                if b is not None:
                    maxima(b, 0)
                if a is not None and c is not None:
                    normal1_stats(a)
                if c is not None:
                    hidden(c, 1)
                if a is not None:
                    normal1(a)
                if c is not None:
                    normal2(c, 1)
                if a is not None:
                    left_k(a)
                    keep_odd_v(a)
                if b is not None:
                    maxima(b, 1)
                    outputs(b, 0)
                if a is not None:
                    rest_of_z(a)
                if c is not None:
                    dve.wait_ge(z2_high, c.count(1, 1))
                    wait(dve, fc_made, c.count(4))
                    ve.tensor_tensor(z2_lo[:], bank0[:], z2_hi[:].bitcast(F32), ALU.subtract).then_inc(z2_split, 1)
                if a is not None:
                    left_q(a)
                if c is not None:
                    parts_of(c, 0)
                    parts_of(c, 1)
                if b is not None:
                    outputs(b, 1)
                if c is not None:
                    parts_of(c, 2)
                    parts_of(c, 3)
                if b is not None:
                    hidden(b, 0)
                    normal2(b, 0)
                if c is not None:
                    dve.wait_ge(mlp_made, c.count(1, 1))
                    dve.wait_ge(hb_made, c.count(2, 2))
                    wait(dve, stored[c.slot], c.loads(16, before=1))
                    ve.tensor_tensor(y[c.slot][:], bank6[:], hb[c.slot][:], ALU.add).then_inc(y_made, 1)
                if b is not None and c is None:
                    dve.wait_ge(w_high, 7)
                    ve.tensor_tensor(proj_lo[:], proj_raw[:], proj_hi[:].bitcast(F32),
                                     ALU.subtract).then_inc(w_split, 1)

            run_steps(dve, first_step, step)

        @block.tensor
        def _(pe):
            mm = nc.tensor.matmul

            def three_pass(out_ap, a_hi, a_lo, b_hi, b_lo, first, last):
                mm(out_ap, a_hi, b_hi, start=first, stop=False, skip_group_check=True)
                mm(out_ap, a_lo, b_hi, start=False, stop=False, skip_group_check=True)
                return mm(out_ap, a_hi, b_lo, start=False, stop=last, skip_group_check=True)

            def by_feature(bank, name, r_hi, r_lo):
                for m in range(KC):
                    cols_m = slice(P * m, P * m + P)
                    for k in range(KC):
                        last = three_pass(bank[:, m, :], w_hi[name][:, k, cols_m], w_lo[name][:, k, cols_m],
                                          r_hi[:, k, :], r_lo[:, k, :], m == 0 and k == 0, k == KC - 1)
                return last

            def turn(bank, src):
                for t in range(TT):
                    for k in range(KC):
                        last = nc.tensor.transpose(bank[:, k, P * t:P * t + P], src[:, t, P * k:P * k + P], ident[:])
                return last

            def score(g, p):
                wait(pe, exped, g.count(4, 2 * p))
                q, k = q_stack[g.slot], k_stack[g.slot]
                for h in range(H):
                    for b in range(2):
                        rows = slice(S * (2 * p + b), S * (2 * p + b) + S)
                        last = mm(scores[S * b:S * b + S, h // 8, S * (h % 8):S * (h % 8) + S],
                                  q[:, head_pos(h), rows], k[:, head_pos(h), rows], start=True, stop=True,
                                  skip_group_check=True)
                last.then_inc(scored, 1)

            def turn_maxima(g, p):
                pe.wait_ge(n_split, g.count(2, p + 1))
                mm(n_t_ps, n_parts[:].rearrange("p k h -> p (k h)"), ident_b[:], start=True, stop=True,
                   skip_group_check=True).then_inc(n_turned, 1)

            def shift(g, p):
                q, k = q_stack[g.slot], k_stack[g.slot]
                pe.wait_ge(n_kept, g.count(2, p + 1))
                for s in range(2):
                    for i in range(4):
                        mm(scores[:, s, P * i:P * i + P], select[:, 4 * s + i, :, :].rearrange("r w k -> r (w k)"),
                           n_t[:], start=(i == 0), stop=False, skip_group_check=True)
                    for i in range(4):
                        for b in range(2):
                            rows = slice(S * (2 * p + b), S * (2 * p + b) + S)
                            for par in range(2):
                                pos = head_pos(2 * (4 * s + i) + par)
                                last = mm(scores[S * par:S * par + S, s, P * i + S * b:P * i + S * b + S],
                                          k[:, pos, rows], q[:, pos, rows], start=False, stop=True,
                                          skip_group_check=True)
                    last.then_inc(shifted, 1)

            def weigh(g, p):
                pe.wait_ge(exped, g.count(4, 2 * p + 2))
                wait(pe, o_made, g.count(2, p))
                for half in range(KC):
                    for b in range(2):
                        cols_b = slice(S * b, S * b + S)
                        for kind in range(2):
                            for i in range(4):
                                hp = 4 * half + i
                                w = ones_bd[:] if kind else v_bd[g.slot][:, 2 * p + b, hp, :, :]
                                last = mm(bank7[32 * i:32 * i + 32, kind, half, cols_b],
                                          w.rearrange("p w d -> p (w d)"), probs[p][:, hp, b, :],
                                          start=True, stop=True, skip_group_check=True)
                last.then_inc(weighed, 1)

            def project(g, p, g_next):
                pe.wait_ge(o_split, g.count(2, p + 1))
                if p == 0:
                    if g_next is not None:
                        pe.wait_ge(q_left, g_next.count(1, 1))
                    bank = bank1
                else:
                    bank = bank5
                for k in range(KC):
                    last = three_pass(bank[:, 0, :], o_hi[:, k, :], o_lo[:, k, :], w_hi["c"][:, k, :],
                                      w_lo["c"][:, k, :], k == 0, k == KC - 1)
                last.then_inc(projected, 1)

            def fc_chunk(g, m):
                bank = fc_bank[m]
                for h in range(2):
                    cols_m = slice(P * (2 * m + h), P * (2 * m + h) + P)
                    for k in range(KC):
                        last = three_pass(bank[:, h, :], fc_hi[:, k, cols_m], fc_lo[:, k, cols_m],
                                          z2_hi[:, k, :], z2_lo[:, k, :], h == 0 and k == 0, k == KC - 1)
                last.then_inc(fc_made, 1)

            def make_k(a):
                pe.wait_ge(ctx_split, a.count(1, 1))
                wait(pe, z2_split, a.count(1, -2))
                by_feature(bank0, "k", ctx_hi, ctx_lo).then_inc(k_made, 1)

            def make_v(a, t):
                if t == 0:
                    wait(pe, y_made, a.count(1, -2))
                rows = slice(P * t, P * t + P)
                for k in range(KC):
                    last = three_pass(bank6[:, t, :], ctx_hi[:, k, rows], ctx_lo[:, k, rows],
                                      w_hi["v"][:, k, :], w_lo["v"][:, k, :], t == 0 and k == 0, k == KC - 1)
                if t == TT - 1:
                    last.then_inc(v_made, 1)

            def turn_z(a):
                pe.wait_ge(z_made, a.count(1, 1))
                wait(pe, hid_made, a.count(2, -3))
                turn(bank1, z).then_inc(z_turned, 1)

            def make_q(a):
                pe.wait_ge(z_split, a.count(1, 1))
                by_feature(bank1, "q", z_hi, z_lo).then_inc(q_made, 1)

            def column_sums(out_cols, w_name_raw, vec, blocks):
                for m in range(blocks):
                    for k in range(KC):
                        last = mm(out_cols[:, m:m + 1], w_name_raw[:, k, P * m:P * m + P],
                                  col[:, COLS[vec] + k:COLS[vec] + k + 1],
                                  start=(m == 0 and k == 0), stop=(k == KC - 1), skip_group_check=True)
                last.then_inc(bias_summed, 1)

            def first_step(a):
                pe.wait_ge(w_split, 1)
                make_k(a)
                pe.wait_ge(col_loaded, 16)
                pe.wait_ge(w_loaded["q"], 16)
                column_sums(bank7[:, 0, 0, 0:KC], w_raw["q"], "ln1_b", KC)
                pe.wait_ge(w_split, 2)
                make_v(a, 0)
                pe.wait_ge(idents_ready, 2)
                turn_z(a)
                make_v(a, 1)
                pe.wait_ge(w_loaded["c"], 16)
                pe.wait_ge(vb_repeated, 1)
                for k in range(KC):
                    last = mm(bank5[:, 0, :], vb_rep[:, k, :], w_raw["c"][:, k, :], start=(k == 0),
                              stop=(k == KC - 1), skip_group_check=True)
                last.then_inc(bias_summed, 1)
                pe.wait_ge(w_split, 3)
                make_q(a)
                pe.wait_ge(w_loaded["fc"], 16)
                pe.wait_ge(bias_ready, 2)
                column_sums(bank5[:, 1, 0:MB], fc_raw, "ln2_b", MB)

            def step(a, b, c):
                if c is None:
                    make_k(a)
                if b is not None:
                    pe.wait_ge(k_stacked[b.slot], b.loads(16 * LOADS_K))
                    pe.wait_ge(q_stacked[b.slot], b.loads(16 * LOADS_Q))
                    score(b, 0)
                if c is not None:
                    project(c, 1, a)
                if a is not None:
                    if c is not None:
                        make_k(a)
                    make_v(a, 0)
                if b is not None:
                    turn_maxima(b, 0)
                if a is not None:
                    make_v(a, 1)
                if b is not None:
                    if c is None:
                        pe.wait_ge(select_set, 1 + PARTS)
                    shift(b, 0)
                if a is not None:
                    turn_z(a)
                if b is not None:
                    score(b, 1)
                    if c is None:
                        pe.wait_ge(v_even_kept, 1)
                        pe.wait_ge(v_odd_kept, 1)
                        pe.wait_ge(ones_ready, 2)
                    weigh(b, 0)
                    turn_maxima(b, 1)
                if c is not None:
                    pe.wait_ge(z2_made, c.count(2, 2))
                    if a is not None:
                        pe.wait_ge(k_left, a.count(1, 1))
                    turn(bank0, z2).then_inc(z2_turned, 1)
                if b is not None:
                    shift(b, 1)
                if a is not None:
                    make_q(a)
                if c is not None:
                    pe.wait_ge(z2_split, c.count(1, 1))
                    if c.c == 0 and isinstance(c.j, int):
                        pe.wait_ge(w_split, 7)
                    fc_chunk(c, 0)
                    pe.wait_ge(hid_made, c.count(2, 2))
                    fc_chunk(c, 1)
                if b is not None:
                    weigh(b, 1)
                if c is not None:
                    for m in (2, 3):
                        pe.wait_ge(gelued, c.count(4, m - 1))
                        fc_chunk(c, m)
                if b is not None:
                    if c is None:
                        pe.wait_ge(w_split, 4)
                    project(b, 0, a)
                if c is not None:
                    if a is not None:
                        pe.wait_ge(v_even_kept, a.count(1, 1))
                        pe.wait_ge(v_odd_kept, a.count(1, 1))
                    else:
                        pe.wait_ge(y_made, c.count(1))
                    for m in range(FC_CHUNKS):
                        pe.wait_ge(g_split, c.count(4, m + 1))
                        for t in range(TT):
                            rows = slice(P * t, P * t + P)
                            for k in (2 * m, 2 * m + 1):
                                last = three_pass(bank6[:, t, :], g_hi[:, k, rows], g_lo[:, k, rows],
                                                  proj_hi[:, k, :], proj_lo[:, k, :], k == 0 and t == 0, k == MB - 1)
                    last.then_inc(mlp_made, 1)

            run_steps(pe, first_step, step)


_INS = ("x", "ctx_t", "mask", "cols", "cproj_b", "proj_b", "q_w", "k_w", "v_w", "cproj_w", "fc_w", "proj_w")


def kernel(**inputs):
    import concourse.bacc as bacc
    from concourse.bass_utils import run_bass_kernel_spmd

    def by_partition(name):
        return np.asarray(inputs["L0_xattn_" + name]).reshape(-1, P).T

    def head_minor(w):
        halves = w.reshape(*w.shape[:-1], KC, P // HD, HD)
        return np.swapaxes(halves, -1, -2).reshape(w.shape)

    inputs = dict(inputs)
    for n in ("q_w", "q_b", "k_w", "k_b"):
        inputs["L0_xattn_" + n] = head_minor(np.asarray(inputs["L0_xattn_" + n]))
    arrays = {
        "x": np.asarray(inputs["x"]).reshape(N, D),
        "ctx_t": np.asarray(inputs["ctx_2048"]).reshape(N, D).T,
        "mask": np.asarray(inputs["mask_BxS2_bf1"]).reshape(N).view(np.uint8),
        "cols": np.concatenate([by_partition(n) for n in COLS], axis=1),
    }
    for n in _INS[4:]:
        arrays[n] = np.asarray(inputs["L0_xattn_" + n])
    arrays = {n: np.ascontiguousarray(arrays[n]) for n in _INS}

    nc = bacc.Bacc("TRN2", target_bir_lowering=False, num_devices=1)
    args = [nc.dram_tensor(f"in_{n}", a.shape, mybir.dt.from_np(a.dtype), kind="ExternalInput").ap()
            for n, a in arrays.items()]
    out = nc.dram_tensor("out", (N, D), F32, kind="ExternalOutput").ap()
    build(nc, *args, out)
    r = run_bass_kernel_spmd(nc, [{f"in_{n}": a for n, a in arrays.items()}], core_ids=[0])
    return r.results[0]["out"].reshape(B, S, D)
```

```python
from contextlib import ExitStack

import numpy as np

import concourse.bass as bass
from concourse import mybir

F32 = mybir.dt.float32
F32R = mybir.dt.float32r
BF16 = mybir.dt.bfloat16
U8 = mybir.dt.uint8
ALU = mybir.AluOpType
ACT = mybir.ActivationFunctionType
AX = mybir.AxisListType

P = 128
B, S, D, H = 32, 64, 256, 16
HD = D // H
INNER = 4 * D
N = B * S
KC = D // P
MB = INNER // P
GT = 256
TT = GT // P
G = N // GT
BG = GT // S
HP = H // 2
EPS = 1e-5
SCALE = 1.0 / float(np.sqrt(np.float32(HD)))
MASKED = -(2.0 ** 100)
PARTS = 3
Q_SLOTS = (0, 0, 0, 1, 1, 2)
K_SLOTS = (0, 1, 2, 0, 1, 0)
MASK_ROW = HD * len(Q_SLOTS)
LOADS_Q = len(Q_SLOTS)
LOADS_K = len(K_SLOTS) + 1
FC_CHUNKS = MB // 2
PAIR_OF_ONES = float(np.array([0x3F803F80], np.uint32).view(np.float32)[0])

COLS = {"ln1_w": 0, "ln1_b": 2, "q_b": 4, "k_b": 6, "v_b": 8, "ln2_w": 10, "ln2_b": 12, "fc_b": 14}
N_COLS = 14 + MB


def head_pos(h):
    return (h % 8) * 2 + h // 8


class Group:

    def __init__(self, j, c):
        self.j, self.c = j, c
        self.slot = c % 2

    def count(self, per_group, k=0):
        const = per_group * self.c + k
        if isinstance(self.j, int):
            return 2 * per_group * self.j + const
        return self.j * (2 * per_group) + const

    def loads(self, per_load, before=0):
        const = per_load * (self.c // 2 + 1 - before)
        if isinstance(self.j, int):
            return per_load * self.j + const
        return self.j * per_load + const

    def start(self):
        return self.count(GT)


def wait(eng, sem, value):
    if isinstance(value, int) and value <= 0:
        return
    eng.wait_ge(sem, value)


def build(nc, x, ctx_t, mask, cols, cproj_b, proj_b, q_w, k_w, v_w, cproj_w, fc_w, proj_w, out):
    x_v = x.rearrange("(g t p) d -> g p t d", p=P, t=TT)
    ctx_v = ctx_t.rearrange("(k p) n -> p k n", p=P)
    x_rows = x.rearrange("(t p) d -> p t d", p=P)
    out_rows = out.rearrange("(t p) d -> p t d", p=P)

    with ExitStack() as stack:
        def sb(name, shape, dt=F32):
            return stack.enter_context(nc.sbuf_tensor(name, shape, dt))

        def psum(name, shape, dt=F32):
            return stack.enter_context(nc.psum_tensor(name, shape, dt))

        def sem(name):
            return stack.enter_context(nc.semaphore(name))

        names = ("q", "k", "v", "c")
        w_raw = {n: sb(f"w_raw_{n}", [P, KC, D]) for n in names}
        w_hi = {n: sb(f"w_hi_{n}", [P, KC, D], F32R) for n in names}
        w_lo = {n: sb(f"w_lo_{n}", [P, KC, D], F32R) for n in names}
        fc_raw = sb("fc_raw", [P, KC, INNER])
        fc_hi = sb("fc_hi", [P, KC, INNER], F32R)
        fc_lo = sb("fc_lo", [P, KC, INNER], F32R)
        proj_raw = sb("proj_raw", [P, MB, D])
        proj_hi = sb("proj_hi", [P, MB, D], F32R)
        proj_lo = sb("proj_lo", [P, MB, D], F32R)
        col = sb("col", [P, N_COLS])
        q_bias = sb("q_bias", [P, KC])
        fc_bias = sb("fc_bias", [P, MB])
        vb_rep = sb("vb_rep", [P, KC, P])
        c_bias = sb("c_bias", [P, D])
        cb_rows = sb("cb_rows", [P, D])
        pb_rows = sb("pb_rows", [P, D])

        ident = sb("ident", [P, P])
        ident_b = sb("ident_b", [P, P], BF16)
        select = sb("select", [PARTS * H, HP, 2, S], BF16)
        ones_bd = sb("ones_bd", [P, 2, HD])
        wait_carrier = sb("wait_carrier", [1, 1])
        table_scratch = sb("table_scratch", [1, 1])
        power = sb("power", [P, TT])
        mask_u8 = sb("mask_u8", [1, N], U8)
        mask_row = sb("mask_row", [1, N], BF16)

        x_in = [sb(f"x_in{s}", [P, TT, D]) for s in range(2)]
        ctx_in = [sb(f"ctx_in{s}", [P, KC, GT]) for s in range(2)]
        ctx_hi = sb("ctx_hi", [P, KC, GT], F32R)
        ctx_lo = sb("ctx_lo", [P, KC, GT], F32R)
        st1 = sb("st1", [P, TT, 6])
        mv1 = sb("mv1", [P, TT, 2])
        ve1 = sb("ve1", [P, TT])
        rs1 = sb("rs1", [P, TT])
        z = sb("z", [P, TT, D])
        z_hi = sb("z_hi", [P, KC, GT], F32R)
        z_lo = sb("z_lo", [P, KC, GT], F32R)
        part = {(n, k): sb(f"part_{n}{k}", [P, KC, GT], BF16) for n in "qk" for k in range(PARTS)}
        rest = {n: sb(f"rest_{n}", [P, KC, GT]) for n in "qk"}
        q_stack = [sb(f"q_stack{s}", [P, H, GT], BF16) for s in range(2)]
        k_stack = [sb(f"k_stack{s}", [P, H, GT], BF16) for s in range(2)]
        v_bd = [sb(f"v_bd{s}", [P, BG, HP, 2, HD]) for s in range(2)]
        xb = [sb(f"xb{s}", [P, TT, D]) for s in range(2)]

        mx = sb("mx", [P, H])
        n_rest = sb("n_rest", [P, H])
        n_parts = sb("n_parts", [P, PARTS, H], BF16)
        n_t = sb("n_t", [PARTS * H, P], BF16)
        probs = [sb(f"probs{p}", [P, HP, 2, S]) for p in range(TT)]
        recip = sb("recip", [P, KC, P])
        o = sb("o", [P, KC, P])
        o_hi = sb("o_hi", [P, KC, P], F32R)
        o_lo = sb("o_lo", [P, KC, P], F32R)
        hid = sb("hid", [P, TT, D])
        hb = [sb(f"hb{s}", [P, TT, D]) for s in range(2)]
        st2 = sb("st2", [P, TT, 6])
        mv2 = sb("mv2", [P, TT, 2])
        ve2 = sb("ve2", [P, TT])
        rs2 = sb("rs2", [P, TT])
        z2 = sb("z2", [P, TT, D])

        z2_hi = sb("z2_hi", [P, KC, GT], F32R)
        z2_lo = sb("z2_lo", [P, KC, GT], F32R)
        gelu = fc_raw[:].rearrange("p k (m t) -> p (k m) t", t=GT)
        g_hi = sb("g_hi", [P, MB, GT], F32R)
        g_lo = sb("g_lo", [P, MB, GT], F32R)
        y = [sb(f"y{s}", [P, TT, D]) for s in range(2)]

        bank0 = psum("bank0", [P, 2, 256])
        bank1 = psum("bank1", [P, 2, 256])
        scores = psum("scores", [P, 2, 512])
        bank4 = psum("bank4", [P, 2, 256])
        bank5 = psum("bank5", [P, 2, 256])
        bank6 = psum("bank6", [P, 2, 256])
        bank7 = psum("bank7", [P, 2, KC, P])
        n_t_ps = bank4[0:PARTS * H, 0, 0:P]

        w_loaded = {n: sem(f"w_loaded_{n}") for n in ("q", "k", "v", "c", "fc", "proj")}
        col_loaded = sem("col_loaded")
        rows_loaded = sem("rows_loaded")
        mask_loaded = sem("mask_loaded")
        x_loaded = [sem(f"x_loaded{s}") for s in range(2)]
        ctx_loaded = [sem(f"ctx_loaded{s}") for s in range(2)]
        q_stacked = [sem(f"q_stacked{s}") for s in range(2)]
        k_stacked = [sem(f"k_stacked{s}") for s in range(2)]
        stored = [sem(f"stored{s}") for s in range(2)]
        idents_zeroed = sem("idents_zeroed")
        idents_ready = sem("idents_ready")
        select_set = sem("select_set")
        ones_zeroed = sem("ones_zeroed")
        ones_ready = sem("ones_ready")
        stacks_set = [sem(f"stacks_set{s}") for s in range(2)]
        v_zeroed = sem("v_zeroed")
        mask_ready = sem("mask_ready")
        vb_repeated = sem("vb_repeated")
        w_high = sem("w_high")
        w_split = sem("w_split")
        bias_summed = sem("bias_summed")
        bias_ready = sem("bias_ready")
        k_made = sem("k_made")
        v_made = sem("v_made")
        z_turned = sem("z_turned")
        q_made = sem("q_made")
        scored = sem("scored")
        n_turned = sem("n_turned")
        shifted = sem("shifted")
        weighed = sem("weighed")
        projected = sem("projected")
        z2_turned = sem("z2_turned")
        fc_made = sem("fc_made")
        mlp_made = sem("mlp_made")
        ctx_high = sem("ctx_high")
        k_lead = sem("k_lead")
        k_second = sem("k_second")
        q_lead = sem("q_lead")
        q_second = sem("q_second")
        v_even_kept = sem("v_even_kept")
        z_high = sem("z_high")
        n_kept = sem("n_kept")
        exped = sem("exped")
        o_high = sem("o_high")
        z2_high = sem("z2_high")
        gelued = sem("gelued")
        maxed = sem("maxed")
        n_lead = sem("n_lead")
        n_left = sem("n_left")
        n_second = sem("n_second")
        n_split = sem("n_split")
        hid_made = sem("hid_made")
        st2_made = sem("st2_made")
        mv2_made = sem("mv2_made")
        var2_made = sem("var2_made")
        z2_made = sem("z2_made")
        st1_made = sem("st1_made")
        mv1_made = sem("mv1_made")
        var1_made = sem("var1_made")
        z_made = sem("z_made")
        k_left = sem("k_left")
        q_left = sem("q_left")
        v_odd_kept = sem("v_odd_kept")
        recip_made = sem("recip_made")
        o_made = sem("o_made")
        z_split = sem("z_split")
        z2_split = sem("z2_split")
        g_high = sem("g_high")
        g_split = sem("g_split")
        y_made = sem("y_made")
        ctx_split = sem("ctx_split")
        rs1_made = sem("rs1_made")
        rs2_made = sem("rs2_made")
        xb_made = sem("xb_made")
        hb_made = sem("hb_made")
        k_third = sem("k_third")
        q_third = sem("q_third")
        o_split = sem("o_split")

        block = stack.enter_context(nc.Block())

        def set_stack(eng, s, stacks, word):
            eng.memset(stacks[s][MASK_ROW:P, :, :].rearrange("p h t -> p (h t)").bitcast(F32), word) \
               .then_inc(stacks_set[s], 1)

        def first_full(c):
            return c.c == 0 and isinstance(c.j, int)

        def late(g):
            return isinstance(g.j, int) and g.count(1) >= G - 2

        def is_last(g):
            return late(g) and g.count(1) == G - 1

        def fc_bank(g, m):
            return (bank5, bank6)[m % 2] if late(g) else (bank4, bank5)[m % 2]

        def mlp_out(g, t):
            if is_last(g) and t:
                return bank7[:, 0, :, :].rearrange("p k t -> p (k t)")
            return (bank4 if late(g) else bank6)[:, t, :]

        def run_steps(eng, first_step, second_step, full_step, last_attention, last_mlp):
            looped_from = 3
            first_step(Group(0, 0))
            second_step(Group(0, 1), Group(0, 0))
            for i in range(1, looped_from):
                full_step(Group(0, i + 1), Group(0, i), Group(0, i - 1))
            with eng.Fori(0, (G - 1 - looped_from) // 2) as j:
                for i in range(looped_from, looped_from + 2):
                    full_step(Group(j, i + 1), Group(j, i), Group(j, i - 1))
            last_attention(Group(0, G - 1), Group(0, G - 2))
            last_mlp(Group(0, G - 1))

        @block.sync
        def _(sp):
            def stack_up(g, name, slots, stacks, stacked, made):
                for k in range(PARTS):
                    sp.wait_ge(made[k], g.count(1, 1))
                    for n in range(len(slots)):
                        if slots[n] == k:
                            sp.dma_start(stacks[g.slot][HD * n:HD * (n + 1), :, :]
                                         .rearrange("r (h m) t -> r h (m t)", m=KC),
                                         part[name, k][:].rearrange("p m t -> p (m t)")) \
                              .then_inc(stacked[g.slot], 16)

            def stack_mask(g):
                sp.dma_start(k_stack[g.slot][MASK_ROW:MASK_ROW + 1, :, :],
                             mask_row[0:1, bass.ds(g.start(), GT)].unsqueeze(1).broadcast_to([1, H, GT])) \
                  .then_inc(k_stacked[g.slot], 16)

            def stack_k(g):
                stack_up(g, "k", K_SLOTS, k_stack, k_stacked, (k_lead, k_second, k_third))

            def stack_q(g):
                stack_up(g, "q", Q_SLOTS, q_stack, q_stacked, (q_lead, q_second, q_third))

            def first_step(a):
                stack_k(a)
                sp.wait_ge(stacks_set[0], 1)
                sp.wait_ge(mask_ready, 1)
                stack_mask(a)
                stack_q(a)

            def second_step(a, b):
                stack_k(a)
                sp.wait_ge(stacks_set[1], 1)
                stack_mask(a)
                load_x(Group(0, 2))
                load_ctx(Group(0, 2))
                stack_q(a)

            def store(c):
                sp.wait_ge(y_made, c.count(1, 1))
                sp.dma_start(out_rows[:, bass.ds(c.count(TT), TT), :], y[c.slot][:]).then_inc(stored[c.slot], 16)

            def full_step(a, b, c, ahead=True):
                sp.wait_ge(shifted, a.count(4, -4))
                stack_mask(a)
                stack_k(a)
                if ahead:
                    load_x(Group(a.j, a.c + 1))
                    load_ctx(Group(a.j, a.c + 1))
                stack_q(a)
                store(c)

            def load_x(g):
                wait(sp, z_made, g.count(1, -1))
                wait(sp, xb_made, g.count(1, -1))
                sp.dma_start(x_in[g.slot][:], x_rows[:, bass.ds(g.count(TT), TT), :]).then_inc(x_loaded[g.slot], 16)

            def load_ctx(g):
                wait(sp, ctx_split, g.count(1, -1))
                sp.dma_start(ctx_in[g.slot][:],
                             ctx_v[:, :, bass.ds(g.start(), GT)]).then_inc(ctx_loaded[g.slot], 16)

            def load_w(name, dst, w):
                sp.dma_start(dst[:], w.rearrange("(k p) n -> p k n", p=P)).then_inc(w_loaded[name], 16)

            def load_row(dst, v):
                sp.dma_start(dst[:], v.rearrange("(a n) -> a n", a=1).broadcast_to([P, D])).then_inc(rows_loaded, 16)

            load_ctx(Group(0, 0))
            load_w("k", w_raw["k"], k_w)
            load_x(Group(0, 0))
            load_w("v", w_raw["v"], v_w)
            sp.dma_start(col[:], cols[:, :]).then_inc(col_loaded, 16)
            load_w("q", w_raw["q"], q_w)
            sp.dma_start(mask_u8[:], mask.rearrange("(a n) -> a n", a=1)).then_inc(mask_loaded, 16)
            load_w("c", w_raw["c"], cproj_w)
            load_row(cb_rows, cproj_b)
            load_w("fc", fc_raw, fc_w)
            load_row(pb_rows, proj_b)
            load_ctx(Group(0, 1))
            load_x(Group(0, 1))
            load_w("proj", proj_raw, proj_w)
            first_step(Group(0, 0))
            second_step(Group(0, 1), Group(0, 0))
            with sp.Fori(0, (G - 4) // 2) as j:
                for c in range(2):
                    full_step(Group(j, c + 2), Group(j, c + 1), Group(j, c))
            full_step(Group(0, G - 2), Group(0, G - 3), Group(0, G - 4))
            full_step(Group(0, G - 1), Group(0, G - 2), Group(0, G - 3), ahead=False)
            store(Group(0, G - 2))
            last = Group(0, G - 1)
            for t in range(TT):
                sp.wait_ge(y_made, last.count(1, 1 + t))
                sp.dma_start(out_rows[:, last.count(TT, t), :], y[last.slot][:, t, :]).then_inc(stored[last.slot], 16)
            sp.wait_ge(stored[0], 16 * (G // 2))
            sp.wait_ge(stored[1], 16 * (G // 2 - 1 + TT))

        @block.gpsimd
        def _(pool):
            gp = nc.gpsimd
            gp.memset(ident[:], 0.0).then_inc(idents_zeroed, 1)
            gp.memset(ident_b[:], 0.0).then_inc(idents_zeroed, 1)
            gp.memset(power[:], -0.5)
            pool.wait_ge(idents_zeroed, 2)
            for t in (ident, ident_b):
                gp.affine_select(out=t[:], in_=t[:], compare_op=ALU.not_equal, fill=1.0, base=0,
                                 pattern=[[-1, P]], channel_multiplier=1).then_inc(idents_ready, 1)

            def set_select():
                gp.memset(select[:], 0.0).then_inc(select_set, 1)
                for k in range(PARTS):
                    pool.wait_ge(select_set, 1 + k)
                    gp.affine_select(out=select[:], in_=select[:], compare_op=ALU.not_equal, fill=1.0, base=-H * k,
                                     pattern=[[-2, HP], [-1, 2], [0, S]], channel_multiplier=1) \
                      .then_inc(select_set, 1)

            def rest_of_ctx(a):
                pool.wait_ge(ctx_loaded[a.slot], a.loads(16))
                wait(pool, v_made, a.count(1))
                pool.wait_ge(ctx_high, a.count(1, 1))
                gp.tensor_tensor(ctx_lo[:], ctx_in[a.slot][:], ctx_hi[:].bitcast(F32),
                                 ALU.subtract).then_inc(ctx_split, 1)

            def scale_1(a):
                pool.wait_ge(var1_made, a.count(1, 1))
                wait(pool, z_made, a.count(1))
                gp.tensor_tensor(rs1[:], ve1[:], power[:], ALU.pow).then_inc(rs1_made, 1)

            def x_and_bias(a):
                pool.wait_ge(x_loaded[a.slot], a.loads(16))
                wait(pool, hid_made, a.count(2, -2))
                gp.tensor_tensor(xb[a.slot][:], x_in[a.slot][:],
                                 c_bias[:].unsqueeze(1).broadcast_to([P, TT, D]), ALU.add).then_inc(xb_made, 1)

            def set_stacks(s, before):
                pool.wait_ge(before, 1)
                set_stack(gp, s, k_stack, 0.0)
                set_stack(gp, s, q_stack, PAIR_OF_ONES)
                pool.wait_ge(stacks_set[s], 2)

            def third_k(a):
                third(a, "k", k_second, k_stacked, 16 * LOADS_K, k_third)

            def third_q(a):
                third(a, "q", q_second, q_stacked, 16 * LOADS_Q, q_third)

            def first_step(a):
                set_select()
                pool.wait_ge(idents_ready, 2)
                scale_1(a)
                set_stacks(0, rs1_made)
                third_k(a)
                gp.memset(v_bd[0][:], 0.0).then_inc(v_zeroed, 1)
                scale_1(Group(0, 1))
                gp.memset(v_bd[1][:], 0.0).then_inc(v_zeroed, 1)
                third_q(a)
                set_stacks(1, q_third)

            def second_step(a, b):
                third_k(a)
                pool.wait_ge(bias_ready, 2)
                x_and_bias(b)
                third_q(a)
                x_and_bias(a)
                rest_of_o(b, 0)
                rest_of_ctx(Group(0, 2))
                rest_of_o(b, 1)

            def full_step(a, b, c):
                if not first_full(c):
                    rest_of_ctx(a)
                scale_1(a)
                row_scale(c, 0)
                row_scale(c, 1)
                keep_hidden(c, 0)
                keep_hidden(c, 1)
                third_k(a)
                x_and_bias(a)
                rest_of_o(b, 0)
                third_q(a)
                rest_of_o(b, 1)

            def last_attention(b, c):
                row_scale(c, 0)
                row_scale(c, 1)
                keep_hidden(c, 0)
                keep_hidden(c, 1)
                rest_of_o(b, 0)
                rest_of_o(b, 1)
                row_scale(b, 0)
                row_scale(b, 1)

            def last_mlp(c):
                keep_hidden(c, 0)
                keep_hidden(c, 1)

            def third(g, n, second, stacked, per_load, made):
                pool.wait_ge(second, g.count(1, 1))
                before = Group(g.j, g.c - 1)
                if not (isinstance(g.j, int) and g.c == 0):
                    wait(pool, stacked[before.slot], before.loads(per_load))
                gp.tensor_tensor(part[n, 2][:], rest[n][:], part[n, 1][:], ALU.subtract).then_inc(made, 1)

            def row_scale(g, p):
                pool.wait_ge(var2_made, g.count(2, p + 1))
                gp.tensor_tensor(rs2[:, p:p + 1], ve2[:, p:p + 1], power[:, 0:1], ALU.pow).then_inc(rs2_made, 1)

            def keep_hidden(g, p):
                pool.wait_ge(hid_made, g.count(2, p + 1))
                if p == 0:
                    wait(pool, y_made, g.count(1, -1))
                gp.tensor_tensor(hb[g.slot][:, p, :], hid[:, p, :], pb_rows[:], ALU.add).then_inc(hb_made, 1)

            def rest_of_o(g, p):
                pool.wait_ge(o_high, g.count(2, p + 1))
                wait(pool, projected, g.count(2, p))
                gp.tensor_tensor(o_lo[:], o[:], o_hi[:].bitcast(F32), ALU.subtract).then_inc(o_split, 1)

            run_steps(pool, first_step, second_step, full_step, last_attention, last_mlp)

        @block.scalar
        def _(act):
            sc = nc.scalar
            def fetch_table(func):
                sc.activation(table_scratch[:], power[0:1, 0:1], func)

            def lead(g, n, made, bank, bias, stacked, per_load, first):
                act.wait_ge(made, g.count(1, 1))
                before = Group(g.j, g.c - 1)
                if not (isinstance(g.j, int) and g.c == 0):
                    wait(act, stacked[before.slot], before.loads(per_load))
                for m in range(KC):
                    last = sc.activation(part[n, 0][:, m, :], bank[:, m, :], ACT.Identity, bias=bias[:, m:m + 1])
                last.then_inc(first, 1)

            def second(g, n, left, made):
                act.wait_ge(left, g.count(1, 1))
                sc.copy(part[n, 1][:], rest[n][:]).then_inc(made, 1)

            def keep_maxima(g, p):
                act.wait_ge(n_turned, g.count(2, p + 1))
                wait(act, shifted, g.count(4, 2 * p))
                sc.copy(n_t[:], n_t_ps).then_inc(n_kept, 1)

            def exp(g, p):
                wait(act, weighed, g.count(2, p - 1))
                for s in range(2):
                    act.wait_ge(shifted, g.count(4, 2 * p + s + 1))
                    sc.activation(probs[p][:, 4 * s:4 * s + 4, :, :],
                                  scores[:, s, :].rearrange("p (h b q) -> p h b q", h=4, b=2),
                                  ACT.Exp, scale=SCALE).then_inc(exped, 1)

            def o_lead(g, p):
                act.wait_ge(o_made, g.count(2, p + 1))
                wait(act, projected, g.count(2, p))
                sc.copy(o_hi[:], o[:]).then_inc(o_high, 1)

            def chunk(g, m):
                act.wait_ge(fc_made, g.count(4, m + 1))
                for h in range(2):
                    last = sc.activation(gelu[:, 2 * m + h, :], fc_bank(g, m)[:, h, :], ACT.Gelu_apprx_tanh,
                                         bias=fc_bias[:, 2 * m + h:2 * m + h + 1])
                last.then_inc(gelued, 1)

            def high(dst, src, count):
                sc.copy(dst[:], src[:]).then_inc(count, 1)

            def high_of_ctx(a):
                act.wait_ge(ctx_loaded[a.slot], a.loads(16))
                wait(act, v_made, a.count(1))
                high(ctx_hi, ctx_in[a.slot], ctx_high)

            def high_of_z2(c):
                act.wait_ge(z2_turned, c.count(1, 1))
                wait(act, fc_made, c.count(4))
                high(z2_hi, bank0, z2_high)

            def keep_even_v(a, zeroed=False):
                act.wait_ge(v_made, a.count(1, 1))
                if zeroed:
                    act.wait_ge(v_zeroed, 2)
                wait(act, weighed, a.count(2, -2))
                for par in range(2):
                    last = sc.copy(
                        v_bd[a.slot][S * par:S * par + S, :, :, par, :]
                        .rearrange("p (t b) h d -> p t b h d", b=2)[:, :, 0, :, :],
                        bank6[0:S, :, :].rearrange("p t (h w d) -> p t h w d", w=2, d=HD)[:, :, :, par, :])
                last.then_inc(v_even_kept, 1)

            def high_of_z(a):
                act.wait_ge(z_turned, a.count(1, 1))
                wait(act, q_made, a.count(1))
                high(z_hi, bank1, z_high)

            def lead_k(a):
                lead(a, "k", k_made, bank0, col[:, COLS["k_b"]:COLS["k_b"] + KC], k_stacked, 16 * LOADS_K, k_lead)

            def lead_q(a):
                lead(a, "q", q_made, bank1, q_bias, q_stacked, 16 * LOADS_Q, q_lead)

            def second_k(a):
                second(a, "k", k_left, k_second)

            def second_q(a):
                second(a, "q", q_left, q_second)

            def first_step(a):
                act.wait_ge(w_loaded["k"], 16)
                high(w_hi["k"], w_raw["k"], w_high)
                high_of_ctx(a)
                act.wait_ge(w_loaded["q"], 16)
                act.wait_ge(col_loaded, 16)
                for k in range(KC):
                    w1 = col[:, COLS["ln1_w"] + k:COLS["ln1_w"] + k + 1]
                    last = sc.activation(w_hi["q"][:, k, :], w_raw["q"][:, k, :], ACT.Copy, scale=w1)
                last.then_inc(w_high, 1)
                act.wait_ge(w_loaded["v"], 16)
                high(w_hi["v"], w_raw["v"], w_high)
                lead_k(a)
                high_of_z(a)
                second_k(a)
                act.wait_ge(bias_ready, 1)
                lead_q(a)
                high_of_ctx(Group(0, 1))
                second_q(a)
                keep_even_v(a, zeroed=True)

            def second_step(a, b):
                lead_k(a)
                high_of_z(a)
                second_k(a)
                act.wait_ge(w_loaded["c"], 16)
                high(w_hi["c"], w_raw["c"], w_high)
                act.wait_ge(w_loaded["fc"], 16)
                for k in range(KC):
                    w2 = col[:, COLS["ln2_w"] + k:COLS["ln2_w"] + k + 1]
                    sc.activation(fc_hi[:, k, :], fc_raw[:, k, :], ACT.Copy, scale=w2).then_inc(w_high, 1)
                lead_q(a)
                second_q(a)
                act.wait_ge(w_loaded["proj"], 16)
                high(proj_hi, proj_raw, w_high)
                act.wait_ge(idents_ready, 2)
                fetch_table(ACT.Exp)
                keep_maxima(b, 0)
                exp(b, 0)
                keep_even_v(a, zeroed=True)
                keep_maxima(b, 1)
                exp(b, 1)
                o_lead(b, 0)
                high_of_ctx(Group(0, 2))
                o_lead(b, 1)

            def full_step(a, b, c):
                if not first_full(c):
                    high_of_ctx(a)
                fetch_table(ACT.Exp)
                keep_maxima(b, 0)
                lead_k(a)
                exp(b, 0)
                high_of_z(a)
                second_k(a)
                keep_maxima(b, 1)
                high_of_z2(c)
                exp(b, 1)
                fetch_table(ACT.Gelu_apprx_tanh)
                keep_even_v(a)
                lead_q(a)
                if first_full(c):
                    act.wait_ge(bias_ready, 3)
                chunk(c, 0)
                second_q(a)
                o_lead(b, 0)
                chunk(c, 1)
                chunk(c, 2)
                o_lead(b, 1)
                chunk(c, 3)

            def last_attention(b, c):
                fetch_table(ACT.Exp)
                keep_maxima(b, 0)
                exp(b, 0)
                high_of_z2(c)
                keep_maxima(b, 1)
                exp(b, 1)
                fetch_table(ACT.Gelu_apprx_tanh)
                chunk(c, 0)
                o_lead(b, 0)
                chunk(c, 1)
                chunk(c, 2)
                o_lead(b, 1)
                chunk(c, 3)

            def last_mlp(c):
                high_of_z2(c)
                for m in range(FC_CHUNKS):
                    chunk(c, m)

            run_steps(act, first_step, second_step, full_step, last_attention, last_mlp)

        @block.vector
        def _(dve):
            ve = nc.vector
            def rest_of_w(name, count):
                dve.wait_ge(w_high, count)
                ve.tensor_tensor(w_lo[name][:], w_raw[name][:], w_hi[name][:].bitcast(F32),
                                 ALU.subtract).then_inc(w_split, 1)
            def carry_wait():
                ve.memset(wait_carrier[:], 0.0)

            def maxima(g, p):
                dve.wait_ge(scored, g.count(2, p + 1))
                ve.reduce_max(mx[:], scores[:, :, :].rearrange("p s (h k) -> p (s h) k", k=S),
                              AX.X).then_inc(maxed, 1)
                dve.wait_ge(maxed, g.count(2, p + 1))
                wait(dve, n_turned, g.count(2, p))
                ve.tensor_scalar(n_parts[:, 0, :], mx[:], -1.0, None, ALU.mult).then_inc(n_lead, 1)
                dve.wait_ge(n_lead, g.count(2, p + 1))
                ve.scalar_tensor_tensor(n_rest[:], mx[:], -1.0, n_parts[:, 0, :],
                                        ALU.mult, ALU.subtract).then_inc(n_left, 1)
                dve.wait_ge(n_left, g.count(2, p + 1))
                ve.tensor_copy(n_parts[:, 1, :], n_rest[:]).then_inc(n_second, 1)
                dve.wait_ge(n_second, g.count(2, p + 1))
                ve.tensor_tensor(n_parts[:, 2, :], n_rest[:], n_parts[:, 1, :], ALU.subtract).then_inc(n_split, 1)

            def hidden(g, p):
                bank = (bank1, bank5)[p]
                dve.wait_ge(projected, g.count(2, p + 1))
                dve.wait_ge(xb_made, g.count(1, 1))
                wait(dve, hb_made, g.count(2, p - 1))
                ve.tensor_tensor(hid[:, p, :], bank[:, 0, :], xb[g.slot][:, p, :], ALU.add).then_inc(hid_made, 1)
                dve.wait_ge(hid_made, g.count(2, p + 1))
                ve.bn_stats(st2[:, p, :], hid[:, p, :]).then_inc(st2_made, 1)

            def variance2(g, p):
                dve.wait_ge(st2_made, g.count(2, p + 1))
                carry_wait()
                ve.bn_aggr(mv2[:, p, :], st2[:, p, :]).then_inc(mv2_made, 1)
                dve.wait_ge(mv2_made, g.count(2, p + 1))
                ve.tensor_scalar(ve2[:, p:p + 1], mv2[:, p, 1:2], EPS, None, ALU.add).then_inc(var2_made, 1)

            def normal2(g, p):
                dve.wait_ge(rs2_made, g.count(2, p + 1))
                wait(dve, z2_turned, g.count(1))
                ve.tensor_scalar(z2[:, p, :], hid[:, p, :], mv2[:, p, 0:1], rs2[:, p:p + 1],
                                 ALU.subtract, ALU.mult).then_inc(z2_made, 1)

            def left(g, n, lead, bank, bias, second, rest_made):
                dve.wait_ge(lead, g.count(1, 1))
                wait(dve, second, g.count(1))
                for m in range(KC):
                    last = ve.scalar_tensor_tensor(rest[n][:, m, :], bank[:, m, :], bias[:, m:m + 1],
                                                   part[n, 0][:, m, :], ALU.add, ALU.subtract)
                last.then_inc(rest_made, 1)

            def outputs(g, p):
                dve.wait_ge(weighed, g.count(2, p + 1))
                ve.reciprocal(recip[:], bank7[:, 1, :, :]).then_inc(recip_made, 1)
                dve.wait_ge(recip_made, g.count(2, p + 1))
                wait(dve, o_split, g.count(2, p))
                ve.tensor_tensor(o[:], bank7[:, 0, :, :], recip[:], ALU.mult).then_inc(o_made, 1)

            def output(c):
                dve.wait_ge(mlp_made, c.count(1, 1))
                dve.wait_ge(hb_made, c.count(2, 2))
                wait(dve, stored[c.slot], c.loads(16, before=1))
                bank = bank4 if late(c) else bank6
                ve.tensor_tensor(y[c.slot][:], bank[:], hb[c.slot][:], ALU.add).then_inc(y_made, 1)

            def parts_of(g, m):
                dve.wait_ge(gelued, g.count(4, m + 1))
                wait(dve, mlp_made, g.count(1))
                ve.tensor_copy(g_hi[:, 2 * m:2 * m + 2, :], gelu[:, 2 * m:2 * m + 2, :]).then_inc(g_high, 1)
                dve.wait_ge(g_high, g.count(4, m + 1))
                ve.tensor_tensor(g_lo[:, 2 * m:2 * m + 2, :], gelu[:, 2 * m:2 * m + 2, :],
                                 g_hi[:, 2 * m:2 * m + 2, :].bitcast(F32), ALU.subtract).then_inc(g_split, 1)

            def stats1(a):
                dve.wait_ge(x_loaded[a.slot], a.loads(16))
                for t in range(TT):
                    last = ve.bn_stats(st1[:, t, :], x_in[a.slot][:, t, :])
                last.then_inc(st1_made, 1)

            def variance1(a):
                dve.wait_ge(st1_made, a.count(1, 1))
                carry_wait()
                for t in range(TT):
                    last = ve.bn_aggr(mv1[:, t, :], st1[:, t, :])
                last.then_inc(mv1_made, 1)
                dve.wait_ge(mv1_made, a.count(1, 1))
                ve.tensor_scalar(ve1[:], mv1[:, :, 1], EPS, None, ALU.add).then_inc(var1_made, 1)

            def normal1(a):
                dve.wait_ge(rs1_made, a.count(1, 1))
                wait(dve, z_turned, a.count(1))
                for t in range(TT):
                    last = ve.tensor_scalar(z[:, t, :], x_in[a.slot][:, t, :], mv1[:, t, 0:1], rs1[:, t:t + 1],
                                            ALU.subtract, ALU.mult)
                last.then_inc(z_made, 1)

            def left_k(a):
                left(a, "k", k_lead, bank0, col[:, COLS["k_b"]:COLS["k_b"] + KC], k_third, k_left)

            def left_q(a):
                left(a, "q", q_lead, bank1, q_bias, q_third, q_left)

            def keep_odd_v(a):
                dve.wait_ge(v_made, a.count(1, 1))
                wait(dve, weighed, a.count(2, -2))
                for par in range(2):
                    last = ve.tensor_copy(
                        v_bd[a.slot][S * par:S * par + S, :, :, par, :]
                        .rearrange("p (t b) h d -> p t b h d", b=2)[:, :, 1, :, :],
                        bank6[S:P, :, :].rearrange("p t (h w d) -> p t h w d", w=2, d=HD)[:, :, :, par, :])
                last.then_inc(v_odd_kept, 1)

            def rest_of_z(a):
                dve.wait_ge(z_high, a.count(1, 1))
                wait(dve, q_made, a.count(1))
                ve.tensor_tensor(z_lo[:], bank1[:], z_hi[:].bitcast(F32), ALU.subtract).then_inc(z_split, 1)

            def rest_of_ctx(a):
                dve.wait_ge(ctx_high, a.count(1, 1))
                wait(dve, v_made, a.count(1))
                ve.tensor_tensor(ctx_lo[:], ctx_in[a.slot][:], ctx_hi[:].bitcast(F32),
                                 ALU.subtract).then_inc(ctx_split, 1)

            def rest_of_z2(c):
                dve.wait_ge(z2_high, c.count(1, 1))
                wait(dve, fc_made, c.count(4))
                ve.tensor_tensor(z2_lo[:], bank0[:], z2_hi[:].bitcast(F32), ALU.subtract).then_inc(z2_split, 1)

            def first_step(a):
                rest_of_w("k", 1)
                rest_of_ctx(a)
                stats1(a)
                variance1(a)
                dve.wait_ge(col_loaded, 16)
                ve.tensor_copy(vb_rep[:], col[:, COLS["v_b"]:COLS["v_b"] + KC].unsqueeze(2)
                               .broadcast_to([P, KC, P])).then_inc(vb_repeated, 1)
                ve.memset(ones_bd[:], 0.0).then_inc(ones_zeroed, 1)
                dve.wait_ge(ones_zeroed, 1)
                for w in range(2):
                    ve.memset(ones_bd[S * w:S * w + S, w, :], 1.0).then_inc(ones_ready, 1)
                normal1(a)
                dve.wait_ge(w_high, 2)
                for k in range(KC):
                    w1 = col[:, COLS["ln1_w"] + k:COLS["ln1_w"] + k + 1]
                    last = ve.scalar_tensor_tensor(w_lo["q"][:, k, :], w_raw["q"][:, k, :], w1,
                                                   w_hi["q"][:, k, :].bitcast(F32), ALU.mult, ALU.subtract)
                last.then_inc(w_split, 1)
                left_k(a)
                rest_of_z(a)
                rest_of_w("v", 3)
                dve.wait_ge(bias_summed, 1)
                ve.tensor_tensor(q_bias[:], bank7[:, 0, 0, 0:KC], col[:, COLS["q_b"]:COLS["q_b"] + KC],
                                 ALU.add).then_inc(bias_ready, 1)
                dve.wait_ge(mask_loaded, 16)
                ve.tensor_scalar(mask_row[:], mask_u8[:], 1.0, -MASKED, ALU.subtract,
                                 ALU.mult).then_inc(mask_ready, 1)
                stats1(Group(0, 1))
                variance1(Group(0, 1))
                left_q(a)
                rest_of_ctx(Group(0, 1))
                normal1(Group(0, 1))
                dve.wait_ge(v_zeroed, 2)
                keep_odd_v(a)
                dve.wait_ge(bias_summed, 2)
                dve.wait_ge(rows_loaded, 32)
                ve.tensor_tensor(c_bias[:], bank5[:, 0, :], cb_rows[:], ALU.add).then_inc(bias_ready, 1)

            def second_step(a, b):
                left_k(a)
                rest_of_z(a)
                rest_of_w("c", 4)
                for k in range(KC):
                    w2 = col[:, COLS["ln2_w"] + k:COLS["ln2_w"] + k + 1]
                    dve.wait_ge(w_high, 5 + k)
                    ve.scalar_tensor_tensor(fc_lo[:, k, :], fc_raw[:, k, :], w2, fc_hi[:, k, :].bitcast(F32),
                                            ALU.mult, ALU.subtract).then_inc(w_split, 1)
                left_q(a)
                maxima(b, 0)
                dve.wait_ge(w_high, 7)
                ve.tensor_tensor(proj_lo[:], proj_raw[:], proj_hi[:].bitcast(F32), ALU.subtract).then_inc(w_split, 1)
                keep_odd_v(a)
                maxima(b, 1)
                outputs(b, 0)
                dve.wait_ge(bias_summed, 3)
                ve.tensor_tensor(fc_bias[:], bank5[:, 1, 0:MB], col[:, COLS["fc_b"]:COLS["fc_b"] + MB],
                                 ALU.add).then_inc(bias_ready, 1)
                outputs(b, 1)
                hidden(b, 0)
                variance2(b, 0)
                maxima(a, 0)

            def full_step(a, b, c):
                stats1(a)
                variance1(a)
                hidden(c, 1)
                normal1(a)
                variance2(c, 1)
                left_k(a)
                normal2(c, 0)
                normal2(c, 1)
                maxima(b, 1)
                rest_of_z(a)
                outputs(b, 0)
                rest_of_z2(c)
                keep_odd_v(a)
                left_q(a)
                parts_of(c, 0)
                parts_of(c, 1)
                outputs(b, 1)
                parts_of(c, 2)
                parts_of(c, 3)
                hidden(b, 0)
                variance2(b, 0)
                maxima(a, 0)
                output(c)

            def last_attention(b, c):
                hidden(c, 1)
                variance2(c, 1)
                normal2(c, 0)
                normal2(c, 1)
                maxima(b, 1)
                rest_of_z2(c)
                outputs(b, 0)
                outputs(b, 1)
                parts_of(c, 0)
                parts_of(c, 1)
                hidden(b, 0)
                variance2(b, 0)
                parts_of(c, 2)
                hidden(b, 1)
                variance2(b, 1)
                normal2(b, 0)
                normal2(b, 1)
                parts_of(c, 3)

            def last_mlp(c):
                rest_of_z2(c)
                output(Group(0, c.c - 1))
                for m in range(FC_CHUNKS):
                    parts_of(c, m)
                dve.wait_ge(stored[c.slot], c.loads(16, before=1))
                for t in range(TT):
                    dve.wait_ge(mlp_made, c.count(1, 1 + t))
                    dve.wait_ge(hb_made, c.count(2, 1 + t))
                    ve.tensor_tensor(y[c.slot][:, t, :], mlp_out(c, t), hb[c.slot][:, t, :],
                                     ALU.add).then_inc(y_made, 1)

            run_steps(dve, first_step, second_step, full_step, last_attention, last_mlp)

        @block.tensor
        def _(pe):
            mm = nc.tensor.matmul

            def three_pass(out_ap, a_hi, a_lo, b_hi, b_lo, first, last):
                mm(out_ap, a_hi, b_hi, start=first, stop=False, skip_group_check=True)
                mm(out_ap, a_lo, b_hi, start=False, stop=False, skip_group_check=True)
                return mm(out_ap, a_hi, b_lo, start=False, stop=last, skip_group_check=True)

            def by_feature(bank, name, r_hi, r_lo):
                for m in range(KC):
                    cols_m = slice(P * m, P * m + P)
                    for k in range(KC):
                        last = three_pass(bank[:, m, :], w_hi[name][:, k, cols_m], w_lo[name][:, k, cols_m],
                                          r_hi[:, k, :], r_lo[:, k, :], m == 0 and k == 0, k == KC - 1)
                return last

            def turn(bank, src):
                for t in range(TT):
                    for k in range(KC):
                        last = nc.tensor.transpose(bank[:, k, P * t:P * t + P], src[:, t, P * k:P * k + P], ident[:])
                return last

            def score(g, p):
                wait(pe, exped, g.count(4, 2 * p))
                q, k = q_stack[g.slot], k_stack[g.slot]
                for h in range(H):
                    for b in range(2):
                        rows = slice(S * (2 * p + b), S * (2 * p + b) + S)
                        last = mm(scores[S * b:S * b + S, h // 8, S * (h % 8):S * (h % 8) + S],
                                  q[:, head_pos(h), rows], k[:, head_pos(h), rows], start=True, stop=True,
                                  skip_group_check=True)
                last.then_inc(scored, 1)

            def turn_maxima(g, p):
                pe.wait_ge(n_split, g.count(2, p + 1))
                mm(n_t_ps, n_parts[:].rearrange("p k h -> p (k h)"), ident_b[:], start=True, stop=True,
                   skip_group_check=True).then_inc(n_turned, 1)

            def shift(g, p):
                q, k = q_stack[g.slot], k_stack[g.slot]
                pe.wait_ge(n_kept, g.count(2, p + 1))
                for s in range(2):
                    for i in range(4):
                        mm(scores[:, s, P * i:P * i + P], select[:, 4 * s + i, :, :].rearrange("r w k -> r (w k)"),
                           n_t[:], start=(i == 0), stop=False, skip_group_check=True)
                    for i in range(4):
                        for b in range(2):
                            rows = slice(S * (2 * p + b), S * (2 * p + b) + S)
                            for par in range(2):
                                pos = head_pos(2 * (4 * s + i) + par)
                                last = mm(scores[S * par:S * par + S, s, P * i + S * b:P * i + S * b + S],
                                          k[:, pos, rows], q[:, pos, rows], start=False, stop=True,
                                          skip_group_check=True)
                    last.then_inc(shifted, 1)

            def weigh(g, p):
                pe.wait_ge(exped, g.count(4, 2 * p + 2))
                wait(pe, o_made, g.count(2, p))
                for half in range(KC):
                    for b in range(2):
                        cols_b = slice(S * b, S * b + S)
                        for kind in range(2):
                            for i in range(4):
                                hp = 4 * half + i
                                w = ones_bd[:] if kind else v_bd[g.slot][:, 2 * p + b, hp, :, :]
                                last = mm(bank7[32 * i:32 * i + 32, kind, half, cols_b],
                                          w.rearrange("p w d -> p (w d)"), probs[p][:, hp, b, :],
                                          start=True, stop=True, skip_group_check=True)
                last.then_inc(weighed, 1)

            def project(g, p, g_next):
                pe.wait_ge(o_split, g.count(2, p + 1))
                if p == 0:
                    if g_next is not None:
                        pe.wait_ge(q_left, g_next.count(1, 1))
                    bank = bank1
                else:
                    bank = bank5
                for k in range(KC):
                    last = three_pass(bank[:, 0, :], o_hi[:, k, :], o_lo[:, k, :], w_hi["c"][:, k, :],
                                      w_lo["c"][:, k, :], k == 0, k == KC - 1)
                last.then_inc(projected, 1)

            def fc_chunk(g, m):
                bank = fc_bank(g, m)
                for h in range(2):
                    cols_m = slice(P * (2 * m + h), P * (2 * m + h) + P)
                    for k in range(KC):
                        last = three_pass(bank[:, h, :], fc_hi[:, k, cols_m], fc_lo[:, k, cols_m],
                                          z2_hi[:, k, :], z2_lo[:, k, :], h == 0 and k == 0, k == KC - 1)
                last.then_inc(fc_made, 1)

            def make_k(a):
                pe.wait_ge(ctx_split, a.count(1, 1))
                wait(pe, z2_split, a.count(1, -2))
                by_feature(bank0, "k", ctx_hi, ctx_lo).then_inc(k_made, 1)

            def make_v(a, t):
                if t == 0:
                    if isinstance(a.j, int) and 0 < a.c < 3:
                        pe.wait_ge(v_even_kept, a.count(1))
                        pe.wait_ge(v_odd_kept, a.count(1))
                    wait(pe, y_made, a.count(1, -2))
                rows = slice(P * t, P * t + P)
                for k in range(KC):
                    last = three_pass(bank6[:, t, :], ctx_hi[:, k, rows], ctx_lo[:, k, rows],
                                      w_hi["v"][:, k, :], w_lo["v"][:, k, :], t == 0 and k == 0, k == KC - 1)
                if t == TT - 1:
                    last.then_inc(v_made, 1)

            def turn_z(a):
                pe.wait_ge(z_made, a.count(1, 1))
                wait(pe, hid_made, a.count(2, -3))
                turn(bank1, z).then_inc(z_turned, 1)

            def turn_z2(c):
                pe.wait_ge(z2_made, c.count(2, 2))
                turn(bank0, z2).then_inc(z2_turned, 1)

            def make_q(a):
                pe.wait_ge(z_split, a.count(1, 1))
                by_feature(bank1, "q", z_hi, z_lo).then_inc(q_made, 1)

            def column_sums(out_cols, w_name_raw, vec, blocks):
                for m in blocks:
                    for k in range(KC):
                        last = mm(out_cols[:, m:m + 1], w_name_raw[:, k, P * m:P * m + P],
                                  col[:, COLS[vec] + k:COLS[vec] + k + 1],
                                  start=(m == 0 and k == 0), stop=(k == KC - 1), skip_group_check=True)
                return last

            def first_step(a):
                pe.wait_ge(w_split, 1)
                make_k(a)
                pe.wait_ge(idents_ready, 2)
                turn_z(a)
                pe.wait_ge(col_loaded, 16)
                pe.wait_ge(w_loaded["q"], 16)
                column_sums(bank7[:, 0, 0, 0:KC], w_raw["q"], "ln1_b", range(KC)).then_inc(bias_summed, 1)
                pe.wait_ge(w_split, 2)
                make_q(a)
                pe.wait_ge(w_split, 3)
                make_v(a, 0)
                make_v(a, 1)
                pe.wait_ge(w_loaded["c"], 16)
                pe.wait_ge(vb_repeated, 1)
                for k in range(KC):
                    last = mm(bank5[:, 0, :], vb_rep[:, k, :], w_raw["c"][:, k, :], start=(k == 0),
                              stop=(k == KC - 1), skip_group_check=True)
                last.then_inc(bias_summed, 1)

            def first_score(g):
                pe.wait_ge(k_stacked[g.slot], g.loads(16 * LOADS_K))
                pe.wait_ge(q_stacked[g.slot], g.loads(16 * LOADS_Q))
                score(g, 0)

            def mlp(g, m, t):
                rows = slice(P * t, P * t + P)
                for k in (2 * m, 2 * m + 1):
                    last = three_pass(mlp_out(g, t), g_hi[:, k, rows], g_lo[:, k, rows],
                                      proj_hi[:, k, :], proj_lo[:, k, :],
                                      k == 0 and (t == 0 or is_last(g)), k == MB - 1)
                return last

            def mlp_chunks(c, chunks):
                for m in chunks:
                    pe.wait_ge(g_split, c.count(4, m + 1))
                    for t in range(TT):
                        last = mlp(c, m, t)
                return last

            def share_of_fc_bias(blocks):
                return column_sums(bank5[:, 1, 0:MB], fc_raw, "ln2_b", blocks)

            def second_step(a, b):
                make_k(a)
                turn_z(a)
                pe.wait_ge(w_loaded["fc"], 16)
                pe.wait_ge(bias_ready, 2)
                share_of_fc_bias(range(0, MB // 2))
                make_q(a)
                pe.wait_ge(stacks_set[0], 2)
                first_score(b)
                make_v(a, 0)
                share_of_fc_bias(range(MB // 2, 3 * MB // 4))
                turn_maxima(b, 0)
                pe.wait_ge(select_set, 1 + PARTS)
                shift(b, 0)
                make_v(a, 1)
                score(b, 1)
                pe.wait_ge(v_even_kept, 1)
                pe.wait_ge(v_odd_kept, 1)
                pe.wait_ge(ones_ready, 2)
                weigh(b, 0)
                turn_maxima(b, 1)
                shift(b, 1)
                share_of_fc_bias(range(3 * MB // 4, MB)).then_inc(bias_summed, 1)
                weigh(b, 1)
                pe.wait_ge(w_split, 4)
                project(b, 0, a)
                pe.wait_ge(stacks_set[1], 2)
                first_score(a)
                make_k(Group(0, 2))
                pe.wait_ge(bias_ready, 3)
                project(b, 1, a)
                pe.wait_ge(w_split, 7)

            def full_step(a, b, c):
                turn_maxima(b, 0)
                if not first_full(c):
                    make_k(a)
                shift(b, 0)
                make_v(a, 0)
                turn_z(a)
                score(b, 1)
                weigh(b, 0)
                make_v(a, 1)
                turn_maxima(b, 1)
                pe.wait_ge(k_left, a.count(1, 1))
                turn_z2(c)
                shift(b, 1)
                make_q(a)
                pe.wait_ge(z2_split, c.count(1, 1))
                fc_chunk(c, 0)
                pe.wait_ge(hid_made, c.count(2, 2))
                fc_chunk(c, 1)
                weigh(b, 1)
                for m in (2, 3):
                    pe.wait_ge(gelued, c.count(4, m - 1))
                    fc_chunk(c, m)
                project(b, 0, a)
                pe.wait_ge(v_even_kept, a.count(1, 1))
                pe.wait_ge(v_odd_kept, a.count(1, 1))
                mlp_chunks(c, (0, 1))
                pe.wait_ge(gelued, c.count(4, 4))
                project(b, 1, a)
                first_score(a)
                mlp_chunks(c, (2, 3)).then_inc(mlp_made, 1)

            def last_attention(b, c):
                turn_maxima(b, 0)
                shift(b, 0)
                score(b, 1)
                turn_z2(c)
                weigh(b, 0)
                turn_maxima(b, 1)
                pe.wait_ge(z2_split, c.count(1, 1))
                fc_chunk(c, 0)
                shift(b, 1)
                pe.wait_ge(y_made, c.count(1))
                fc_chunk(c, 1)
                weigh(b, 1)
                for m in (2, 3):
                    pe.wait_ge(gelued, c.count(4, m - 1))
                    fc_chunk(c, m)
                project(b, 0, None)
                mlp_chunks(c, (0,))
                pe.wait_ge(gelued, c.count(4, 3))
                project(b, 1, None)
                mlp_chunks(c, (1, 2))
                turn_z2(b)
                mlp_chunks(c, (3,)).then_inc(mlp_made, 1)

            def last_mlp(c):
                pe.wait_ge(z2_split, c.count(1, 1))
                for m in range(FC_CHUNKS):
                    if m >= 2:
                        pe.wait_ge(gelued, c.count(4, m - 1))
                    fc_chunk(c, m)
                pe.wait_ge(y_made, c.count(1))
                for t in range(TT):
                    for m in range(FC_CHUNKS):
                        pe.wait_ge(g_split, c.count(4, m + 1))
                        last = mlp(c, m, t)
                    last.then_inc(mlp_made, 1)

            run_steps(pe, first_step, second_step, full_step, last_attention, last_mlp)


_INS = ("x", "ctx_t", "mask", "cols", "cproj_b", "proj_b", "q_w", "k_w", "v_w", "cproj_w", "fc_w", "proj_w")


def kernel(**inputs):
    import concourse.bacc as bacc
    from concourse.bass_utils import run_bass_kernel_spmd

    def by_partition(name):
        return np.asarray(inputs["L0_xattn_" + name]).reshape(-1, P).T

    def head_minor(w):
        halves = w.reshape(*w.shape[:-1], KC, P // HD, HD)
        return np.swapaxes(halves, -1, -2).reshape(w.shape)

    inputs = dict(inputs)
    for n in ("q_w", "q_b", "k_w", "k_b"):
        inputs["L0_xattn_" + n] = head_minor(np.asarray(inputs["L0_xattn_" + n]))
    arrays = {
        "x": np.asarray(inputs["x"]).reshape(N, D),
        "ctx_t": np.asarray(inputs["ctx_2048"]).reshape(N, D).T,
        "mask": np.asarray(inputs["mask_BxS2_bf1"]).reshape(N).view(np.uint8),
        "cols": np.concatenate([by_partition(n) for n in COLS], axis=1),
    }
    for n in _INS[4:]:
        arrays[n] = np.asarray(inputs["L0_xattn_" + n])
    arrays = {n: np.ascontiguousarray(arrays[n]) for n in _INS}

    nc = bacc.Bacc("TRN2", target_bir_lowering=False, num_devices=1)
    args = [nc.dram_tensor(f"in_{n}", a.shape, mybir.dt.from_np(a.dtype), kind="ExternalInput").ap()
            for n, a in arrays.items()]
    out = nc.dram_tensor("out", (N, D), F32, kind="ExternalOutput").ap()
    build(nc, *args, out)
    r = run_bass_kernel_spmd(nc, [{f"in_{n}": a for n, a in arrays.items()}], core_ids=[0])
    return r.results[0]["out"].reshape(B, S, D)
```
